# Optimizing a Trainium2 kernel written in Bass

```python
import numpy as np
import jax
import jax.numpy as jnp

def _softmax(x, axis=-1):
    return jax.nn.softmax(x, axis=axis)

def _gelu(x):
    return jax.nn.gelu(x, approximate=True)

def _silu(x):
    return jax.nn.silu(x)

def _sigmoid(x):
    return jax.nn.sigmoid(x)

def _layernorm(x, axis=-1, eps=1e-05):
    m = jnp.mean(x, axis=axis, keepdims=True)
    v = jnp.var(x, axis=axis, keepdims=True)
    return (x - m) / jnp.sqrt(v + eps)

def _scatter_add(tgt, idx, src, axis=0):
    return tgt.at[idx].add(src)

def _segment_sum(src, seg, n):
    return jax.ops.segment_sum(src, seg, n)
kernel_name = 'mk_gps_d1_gnn_r8_34173e'

def setup_inputs(seed: int=0):
    np.random.seed(seed)
    _w = jnp.asarray

    def _rec_inputs():
        import jax
        import jax.numpy as jnp
        _gk = jax.random.key(seed)
        x = -8.776e-05 + 1 * jax.random.normal(jax.random.fold_in(_gk, 1), (1250, 512), jnp.float32)
        src = jax.random.randint(jax.random.fold_in(_gk, 2), (20000,), 0, 1250, jnp.int32)
        dst = jnp.minimum((1250 * jax.random.uniform(jax.random.fold_in(_gk, 3), (20000,)) ** 2.0).astype(jnp.int32), 9999)
        _o = jnp.argsort(dst, stable=True)
        src = src[_o]
        dst = dst[_o]
        return (x, src, dst)
    x, src, dst = _rec_inputs()

    def _L0_gnn_setup():
        import jax, jax.numpy as jnp
        import numpy as np
        N_NODES = 1250
        N_EDGES = 20000
        D_IN = 512
        D_OUT = 512
        LEAKY_SLOPE = 0.01
        EPS = 1e-12
        key = jax.random.key(seed)
        k1, k2, k3, k4, k5, k6 = jax.random.split(key, 6)
        x = jax.random.normal(k1, (N_NODES, D_IN), dtype=jnp.float32)
        src = jax.random.randint(k2, (N_EDGES,), 0, N_NODES, dtype=jnp.int64)
        dst = jax.random.randint(k3, (N_EDGES,), 0, N_NODES, dtype=jnp.int64)
        scale = 1.0 / np.sqrt(D_IN)
        W_self = jax.random.normal(k4, (D_IN, D_OUT), dtype=jnp.float32) * scale
        W_neigh = jax.random.normal(k5, (D_IN, D_OUT), dtype=jnp.float32) * scale
        b = jax.random.normal(k6, (D_OUT,), dtype=jnp.float32) * scale
        return {'x': x, 'src': src, 'dst': dst, 'W_self': W_self, 'W_neigh': W_neigh, 'b': b}
    _L0_gnn_all = _L0_gnn_setup()
    _L0_gnn_in = {k: v for k, v in _L0_gnn_all.items() if k in ('W_self', 'W_neigh', 'b')}
    del _L0_gnn_all

    def _L0_mix_setup():
        import jax, jax.numpy as jnp
        import numpy as np
        B, N, C = (8, 1024, 512)
        H = 8
        D = C // H
        EPS = 1e-06

        def _linear_attention(q, k, v):
            qf = jax.nn.elu(q) + 1.0
            kf = jax.nn.elu(k) + 1.0
            kv = jnp.einsum('bhnd,bhne->bhde', kf, v)
            z = jnp.einsum('bhnd,bhd->bhn', qf, kf.sum(axis=2))
            out = jnp.einsum('bhnd,bhde->bhne', qf, kv) / (z[..., None] + EPS)
            return out
        key = jax.random.key(seed)
        k1, k2, k3, k4 = jax.random.split(key, 4)
        x = jax.random.normal(k1, (B, N, C), dtype=jnp.float32)
        w_qkv = jax.random.normal(k2, (C, 3 * C), dtype=jnp.float32) * (1.0 / np.sqrt(C))
        w_proj = jax.random.normal(k3, (C, C), dtype=jnp.float32) * (1.0 / np.sqrt(C))
        b_proj = jax.random.normal(k4, (C,), dtype=jnp.float32) * 0.01
        return {'x': x, 'w_qkv': w_qkv, 'w_proj': w_proj, 'b_proj': b_proj}
    _L0_mix_all = _L0_mix_setup()
    _L0_mix_in = {k: v for k, v in _L0_mix_all.items() if k in ('w_qkv', 'w_proj', 'b_proj')}
    del _L0_mix_all

    def _L0_ffn_setup():
        import jax, jax.numpy as jnp
        import numpy as np
        DIM = 512
        FFN_DIM = 1408
        GROUP = 128
        EPS = 1e-05

        def _quantize_weight(w, group_size):
            o, i = w.shape
            wg = w.reshape(o, i // group_size, group_size)
            scale = jnp.mean(jnp.abs(wg), axis=-1, keepdims=True) + EPS
            wq = jnp.clip(jnp.round(wg / scale), -1.0, 1.0) * scale
            return wq.reshape(o, i)

        def _bitlinear(x, w, group_size=GROUP):
            wq = w + jax.lax.stop_gradient(_quantize_weight(w, group_size) - w)
            return jnp.einsum('bsd,fd->bsf', x, wq)
        key = jax.random.key(seed)
        k_x, k_g, k_u, k_d = jax.random.split(key, 4)
        x = jax.random.normal(k_x, (8, 512, DIM), dtype=jnp.float32)
        sd_in = 1.0 / np.sqrt(DIM)
        sd_ffn = 1.0 / np.sqrt(FFN_DIM)
        w_gate = jax.random.normal(k_g, (FFN_DIM, DIM), dtype=jnp.float32) * sd_in
        w_up = jax.random.normal(k_u, (FFN_DIM, DIM), dtype=jnp.float32) * sd_in
        w_down = jax.random.normal(k_d, (DIM, FFN_DIM), dtype=jnp.float32) * sd_ffn
        return {'x': x, 'w_gate': w_gate, 'w_up': w_up, 'w_down': w_down}
    _L0_ffn_all = _L0_ffn_setup()
    _L0_ffn_in = {k: v for k, v in _L0_ffn_all.items() if k in ('w_gate', 'w_up', 'w_down')}
    del _L0_ffn_all
    return {'x': x, 'src': src, 'dst': dst, 'L0_gnn_W_self': _L0_gnn_in['W_self'], 'L0_gnn_W_neigh': _L0_gnn_in['W_neigh'], 'L0_gnn_b': _L0_gnn_in['b'], 'L0_mix_w_qkv': _L0_mix_in['w_qkv'], 'L0_mix_w_proj': _L0_mix_in['w_proj'], 'L0_mix_b_proj': _L0_mix_in['b_proj'], 'L0_ffn_w_gate': _L0_ffn_in['w_gate'], 'L0_ffn_w_up': _L0_ffn_in['w_up'], 'L0_ffn_w_down': _L0_ffn_in['w_down']}

def reference(x, src, dst, L0_gnn_W_self, L0_gnn_W_neigh, L0_gnn_b, L0_mix_w_qkv, L0_mix_w_proj, L0_mix_b_proj, L0_ffn_w_gate, L0_ffn_w_up, L0_ffn_w_down):
    import jax
    import jax.numpy as jnp

    def _L0_gnn_ref(x, src, dst, W_self, W_neigh, b):
        import jax, jax.numpy as jnp
        import numpy as np
        N_NODES = 1250
        N_EDGES = 20000
        D_IN = 512
        D_OUT = 512
        LEAKY_SLOPE = 0.01
        EPS = 1e-12
        msg_sum = jax.ops.segment_sum(x[src], dst, num_segments=N_NODES)
        deg = jax.ops.segment_sum(jnp.ones((src.shape[0],), x.dtype), dst, num_segments=N_NODES)
        neigh = msg_sum / jnp.maximum(deg, 1.0)[:, None]
        h = x @ W_self + neigh @ W_neigh + b
        h = jnp.where(h >= 0, h, LEAKY_SLOPE * h)
        norm = jnp.sqrt(jnp.sum(h * h, axis=1, keepdims=True))
        return h / jnp.maximum(norm, EPS)

    def _L0_mix_ref(x, w_qkv, w_proj, b_proj):
        import jax, jax.numpy as jnp
        import numpy as np
        B, N, C = (8, 1024, 512)
        H = 8
        D = C // H
        EPS = 1e-06

        def _linear_attention(q, k, v):
            qf = jax.nn.elu(q) + 1.0
            kf = jax.nn.elu(k) + 1.0
            kv = jnp.einsum('bhnd,bhne->bhde', kf, v)
            z = jnp.einsum('bhnd,bhd->bhn', qf, kf.sum(axis=2))
            out = jnp.einsum('bhnd,bhde->bhne', qf, kv) / (z[..., None] + EPS)
            return out
        b, n, c = x.shape
        qkv = x @ w_qkv
        qkv = qkv.reshape(b, n, 3, H, D).transpose(2, 0, 3, 1, 4)
        q, k, v = (qkv[0], qkv[1], qkv[2])
        attn = _linear_attention(q, k, v)
        y = attn.transpose(0, 2, 1, 3).reshape(b, n, c)
        return y @ w_proj + b_proj

    def _L0_ffn_ref(x, w_gate, w_up, w_down):
        import jax, jax.numpy as jnp
        import numpy as np
        DIM = 512
        FFN_DIM = 1408
        GROUP = 128
        EPS = 1e-05

        def _quantize_weight(w, group_size):
            o, i = w.shape
            wg = w.reshape(o, i // group_size, group_size)
            scale = jnp.mean(jnp.abs(wg), axis=-1, keepdims=True) + EPS
            wq = jnp.clip(jnp.round(wg / scale), -1.0, 1.0) * scale
            return wq.reshape(o, i)

        def _bitlinear(x, w, group_size=GROUP):
            wq = w + jax.lax.stop_gradient(_quantize_weight(w, group_size) - w)
            return jnp.einsum('bsd,fd->bsf', x, wq)
        gate = _bitlinear(x, w_gate)
        up = _bitlinear(x, w_up)
        h = jax.nn.silu(gate) * up
        return _bitlinear(h, w_down)
    xn = _layernorm(x, axis=-1)
    x = x + _L0_gnn_ref(xn, src, dst, L0_gnn_W_self, L0_gnn_W_neigh, L0_gnn_b) + _L0_mix_ref(xn[None], L0_mix_w_qkv, L0_mix_w_proj, L0_mix_b_proj)[0]
    x = x + _L0_ffn_ref(_layernorm(x, axis=-1)[None], L0_ffn_w_gate, L0_ffn_w_up, L0_ffn_w_down)[0]
    return x

_drawn_inputs = setup_inputs


def setup_inputs(seed=0):
    import zlib

    import numpy as np

    out = dict(_drawn_inputs(seed))
    spreads = {}
    factors = {'L0_gnn_W_neigh': 4.58, 'L0_gnn_b': 8.0, 'L0_mix_b_proj': 5.95}
    for name, (base, spread) in spreads.items():
        noise = np.random.default_rng([zlib.crc32(name.encode()), seed]).standard_normal(out[name].shape)
        drawn = base * np.exp(spread * noise) if base else spread * noise
        out[name] = jnp.asarray(drawn.astype(out[name].dtype))
    for name, factor in factors.items():
        out[name] = (out[name] * factor).astype(out[name].dtype)
    return out
```

```python
from contextlib import ExitStack

import concourse.bass as bass
from concourse import mybir

F32 = mybir.dt.float32
F32R = mybir.dt.float32r
F16 = mybir.dt.float16
I32 = mybir.dt.int32
ALU = mybir.AluOpType
ACT = mybir.ActivationFunctionType
AX_X = mybir.AxisListType.X

P = 128
N = 1250
D = 512
KC = D // P
NT = (N + P - 1) // P
ROWS = [min(P, N - i * P) for i in range(NT)]
CHUNKS = [(0, 512), (512, 1024), (1024, N)]
CH = len(CHUNKS)
TILES_PER_CHUNK = 512 // P
HEAD = 64
EDGES = 20000
UNIT = 250
UK = UNIT // 2
UNITS = EDGES // UNIT
SRC_W = NT * P
FFN = 1408
FT = FFN // P
UNITS_W = 3 * FT
LN_EPS = 1e-5
Q_EPS = 1e-5
Z_EPS = 1e-6
NORM_EPS = 1e-12
SLOPE = 0.01
BIG = 999.0

PASSES = [(0, 0), (0, 1), (1, 0)]


def gnn_mix_ffn_kernel(nc, x, src, dst, W_self, W_neigh, b, w_qkv, w_proj, b_proj, w_gate, w_up, w_down, out):
    ctx = ExitStack()
    with ctx:
        arena = 16512

        def at(name, shape, dt, offset):
            return nc.alloc_sbuf_tensor_at(name, shape, dt, offset=arena + offset)

        def sem(name):
            return ctx.enter_context(nc.semaphore(name))

        x_sb = at("x_sb", [P, NT, D], F32, 0)
        XT = 20480
        xnT = [at("xnT_h", [P, KC, N], F32R, XT), at("xnT_l", [P, KC, N], F32R, XT + 20000)]
        wdT = [[None] * FT, [None] * FT]
        WB = 60544
        raw_w = at("raw_w", [P, 2, KC, D], F32, WB)
        WS = WB + 16384
        w_hl = [[at(f"w_{'hl'[q]}{s}", [P, KC, D], F32R, WS + 16384 * s + 8192 * q) for q in (0, 1)] for s in range(3)]
        R1 = WS + 3 * 16384
        yT = [at("yT_h", [P, KC, N], F32R, R1), at("yT_l", [P, KC, N], F32R, R1 + 20000)]
        pn = [at("pn_h", [P, NT, D], F32R, R1), at("pn_l", [P, NT, D], F32R, R1 + 20480)]
        R2 = R1 + 40960
        qfT = at("qfT", [P, KC, N], F32, R2)
        self_sb = at("self_sb", [P, NT, D], F32, R2)
        iota = at("iota", [P, SRC_W], F16, WS)
        zero16 = at("zero16", [P, 512], F16, WS + 2560)
        ones16 = at("ones16", [P, 2], F16, WS + 3584)
        src_hot = at("src_hot", [P, 2, SRC_W], F16, WS + 3616)
        dst_hot = at("dst_hot", [P, 2, P], F16, WS + 8736)
        cnt = [[at(f"cnt_{'hl'[q]}{s}", [P, NT, P], F32R, WS + 16384 + 5120 * (2 * s + q)) for q in (0, 1)]
               for s in (0, 1)]
        hT = [at("hT_h", [P, FT, N], F32R, WB), at("hT_l", [P, FT, N], F32R, WB + 55008)]
        WT = WB + 2 * 55008
        guT = [[at(f"guT_{'hl'[q]}{s}", [P, KC, P], F32R, WT + 4096 * s + 2048 * q) for q in (0, 1)] for s in range(4)]
        for j in range(FT):
            base = XT + 4096 * j if j < 9 else WT + 4096 * (j - 9)
            for q in (0, 1):
                wdT[q][j] = at(f"wdT_{'hl'[q]}{j}", [P, D], F32R, base + 2048 * q)
        C0 = R2 + 20480
        kf = at("kf", [P, 2, D], F32, C0)
        ex = at("ex", [P, 2, D], F32, C0 + 4096)
        vx = at("vx", [P, 2, KC, P + 2], F32, C0 + 8192)
        xn = at("xn", [P, 2, D], F32, C0 + 8192 + 4160)
        raw_f = at("raw_f", [P, 3, KC, P], F32, C0)
        q_f = at("q_f", [P, 2, KC, P], F32, C0 + 6144)
        act_f = at("act_f", [P, 3, 512], F32, C0 + 10240)
        C1 = C0 + 16448
        b_bc = at("b_bc", [P, D], F32, C1)
        bp_bc = at("bp_bc", [P, D], F32, C1 + 2048)
        edge = at("edge", [P, 2, 2, UNITS], F32, C1 + 4096)
        ident = at("ident", [P, P], F32, C1 + 5376)
        small = C1 + 5888
        stats = at("stats", [P, 2, 6], F32, small)
        mv = at("mv", [P, NT, 2], F32, small + 64)
        rstd = at("rstd", [P, NT], F32, small + 160)
        mv2 = at("mv2", [P, 2, 2], F32, small + 224)
        col = at("col", [P, 16], F32, small + 256)
        scal = at("scal", [P, 2, 3, KC], F32, small + 320)
        rdeg = at("rdeg", [P, NT], F32, small + 416)
        eps_c = at("eps_c", [P, 1], F32, small + 480)
        kvb = at("kvb", [P, KC, P], F32, C0 + 8192)
        ksb = at("ksb", [P, KC, P], F32, C0 + 8192 + 2048)
        E0 = R1 + 20480
        edge_i = at("edge_i", [UNITS, 2, UNIT], I32, E0)
        edge_f = at("edge_f", [UNITS, 2, UNIT], F32, E0 + 2048)
        rng = at("rng", [UNITS, 2], F32, E0 + 4096)
        win = at("win", [NT, 6, UNITS], F32, E0 + 4160)
        wcol = at("wcol", [NT, 8], F32, E0 + 6144)
        prefix = at("prefix", [NT, NT + 1], F32, E0 + 6208)
        unit_m = at("unit_m", [NT, 2, UNITS], F32, E0 + 6272)
        thr = at("thr", [NT, 1], F32, E0 + 6976)
        wrow = at("wrow", [1, 2, 16], F32, E0 + 7008)
        wreg = at("wreg", [1, 2, 16], I32, small + 512)

        ps = ctx.enter_context(nc.psum_tensor("ps", [P, 8, 512], F32))

        x_in = [sem(f"x_in{g}") for g in range(3)]
        raw_in = [sem(f"raw_in{s}") for s in range(2)]
        bias_in = sem("bias_in")
        edge_in = sem("edge_in")
        consts = sem("consts")
        eps_set = sem("eps_set")
        stat_done = sem("stat_done")
        std_done = sem("std_done")
        xn_ready = sem("xn_ready")
        t_done = sem("t_done")
        th_ready = sem("th_ready")
        xnT_ready = sem("xnT_ready")
        wh_ready = sem("wh_ready")
        w_ready = sem("w_ready")
        w_used = sem("w_used")
        xb_ready = sem("xb_ready")
        k_done, v_done, acc_done = sem("k_done"), sem("v_done"), sem("acc_done")
        ek_ready = sem("ek_ready")
        kf_ready, v_ready = sem("kf_ready"), sem("v_ready")
        kvb_ready = sem("kvb_ready")
        kv_zero = sem("kv_zero")
        e_f32 = sem("e_f32")
        e_t, e_copied, e_bc, e_win, e_row, e_reg = (sem("e_t"), sem("e_copied"), sem("e_bc"), sem("e_win"),
                                                   sem("e_row"), sem("e_reg"))
        q_done, qf_ready = sem("q_done"), sem("qf_ready")
        nz_done, y_ready, yh_ready, yl_ready = sem("nz_done"), sem("y_ready"), sem("yh_ready"), sem("yl_ready")
        mix_done, mix_added = sem("mix_done"), sem("mix_added")
        p_done, ph_ready, p_ready = sem("p_done"), sem("ph_ready"), sem("p_ready")
        s_done, s_ready = sem("s_done"), sem("s_ready")
        gnn_const = sem("gnn_const")
        hot_free, hot_ready = sem("hot_free"), sem("hot_ready")
        a_done, ah_ready, a_ready = sem("a_done"), sem("ah_ready"), sem("a_ready")
        msg_done, g_read, h_ready, ss_ready, nrm_ready = (sem("msg_done"), sem("g_read"), sem("h_ready"),
                                                         sem("ss_ready"), sem("nrm_ready"))
        st2_ready, sd2_ready, xn2_ready = sem("st2_ready"), sem("sd2_ready"), sem("xn2_ready")
        t2_done, t2h_ready, xn2T_ready = sem("t2_done"), sem("t2h_ready"), sem("xn2T_ready")
        f_in = [sem(f"f_in{s}") for s in range(3)]
        qa_ready, q_ready = sem("qa_ready"), sem("q_ready")
        ft_done, fh_ready, fw_ready = sem("ft_done"), sem("fh_ready"), sem("fw_ready")
        gu_done, silu_ready, hid_ready, hh_ready, hl_ready = (sem("gu_done"), sem("silu_ready"), sem("hid_ready"),
                                                             sem("hh_ready"), sem("hl_ready"))
        ffn1_done = sem("ffn1_done")
        down_done, y_final = sem("down_done"), sem("y_final")
        out_done = sem("out_done")
        dve_step, act_step, pool_step = sem("dve_step"), sem("act_step"), sem("pool_step")

        X_LOADS = [(0, 2), (2, NT - 1), (NT - 1, NT)]
        K_, V_, Q_, PROJ_, NEIGH_, SELF_ = range(6)
        W_BLOCKS = [w_qkv[:, D:2 * D], w_qkv[:, 2 * D:3 * D], w_qkv[:, 0:D], w_proj, W_neigh, W_self]

        def w_of(block, q):
            return w_hl[block % 3][q]

        T_BANK, K_BANK, V_BANK, ACC_BANK = 0, 2, 4, 6
        A_BANK, MSG_BANK = 5, 2
        PE_GU = 2

        def cols(i):
            return slice(i * P, i * P + ROWS[i])

        def counts_ps(width):
            return ps[:, A_BANK:A_BANK + 3, :].rearrange("p b n -> p (b n)")[:, 0:width]

        DEG = SRC_W

        def ffn_weight(u):
            if u < 2 * FT:
                w = (w_gate, w_up)[u % 2]
                return w[(u // 2) * P:(u // 2 + 1) * P, :].rearrange("p (k n) -> p k n", k=KC)
            j = u - 2 * FT
            return w_down.rearrange("(c p) f -> p c f", p=P)[:, :, j * P:(j + 1) * P]

        def ffn_weight_T(u, q):
            if u < 2 * FT:
                return guT[u % 4][q][:, :, :]
            return wdT[q][u - 2 * FT][:, :].rearrange("p (c n) -> p c n", c=KC)

        DOWN_A = 6
        LEAD = 2

        block = ctx.enter_context(nc.Block())

        @block.sync
        def _(sp):
            for g, (i0, i1) in enumerate(X_LOADS):
                if g == 1:
                    sp.dma_start(raw_w[:, 0], W_BLOCKS[0].rearrange("(k p) n -> p k n", p=P)).then_inc(raw_in[0], 16)
                if i1 < NT:
                    sp.dma_start(x_sb[:, i0:i1, :], x[i0 * P:i1 * P, :].rearrange("(i p) n -> p i n", p=P)
                                 ).then_inc(x_in[g], 16)
                else:
                    sp.dma_start(x_sb[0:ROWS[-1], i0, :], x[i0 * P:N, :]).then_inc(x_in[g], 16)
            for blk in range(1, 6):
                if blk == 2:
                    sp.dma_start(bp_bc[:, :], b_proj.partition_broadcast(P)).then_inc(bias_in, 16)
                    sp.dma_start(b_bc[:, :], b.partition_broadcast(P)).then_inc(bias_in, 16)
                    sp.dma_start(edge_i[:, 0, :], src.rearrange("(m e) -> m e", e=UNIT)).then_inc(edge_in, 16)
                    sp.dma_start(edge_i[:, 1, :], dst.rearrange("(m e) -> m e", e=UNIT)).then_inc(edge_in, 16)
                if blk >= 2:
                    sp.wait_ge(w_ready, blk - 1)
                sp.dma_start(raw_w[:, blk % 2], W_BLOCKS[blk].rearrange("(k p) n -> p k n", p=P)
                             ).then_inc(raw_in[blk % 2], 16)
            sp.wait_ge(t2_done, NT)
            for u in range(UNITS_W):
                if u >= 3:
                    sp.wait_ge(q_ready, u - 2)
                sp.dma_start(raw_f[:, u % 3], ffn_weight(u)).then_inc(f_in[u % 3], 16)
            for i in range(NT):
                sp.wait_ge(y_final, i + 1)
                sp.dma_start(out[i * P:i * P + ROWS[i], :], x_sb[0:ROWS[i], i, :]).then_inc(out_done, 16)
            sp.wait_ge(out_done, 16 * NT)

        @block.gpsimd
        def _(pool):
            steps = [0]

            def step(ins):
                steps[0] += 1
                ins.then_inc(pool_step, 1)
                pool.wait_ge(pool_step, steps[0])

            step(pool.iota(ident[:, :], pattern=[[1, P]], base=0, channel_multiplier=-1,
                           allow_small_or_imprecise_dtypes=True))
            pool.tensor_scalar(ident[:, :], ident[:, :], 0.0, None, ALU.is_equal).then_inc(consts, 1)
            pool.memset(vx[:, :, :, P:P + 2], 1.0).then_inc(consts, 1)
            step(pool.iota(prefix[:, :], pattern=[[1, NT + 1]], base=0, channel_multiplier=-1,
                           allow_small_or_imprecise_dtypes=True))
            pool.tensor_scalar(prefix[:, :], prefix[:, :], 0.0, None, ALU.is_gt).then_inc(consts, 1)
            pool.iota(thr[:, :], pattern=[[0, 1]], base=0, channel_multiplier=P,
                      allow_small_or_imprecise_dtypes=True).then_inc(consts, 1)
            pool.iota(unit_m[:, 0, :], pattern=[[1, UNITS]], base=-int(BIG), channel_multiplier=0,
                      allow_small_or_imprecise_dtypes=True).then_inc(consts, 1)
            pool.iota(unit_m[:, 1, :], pattern=[[1, UNITS]], base=1, channel_multiplier=0,
                      allow_small_or_imprecise_dtypes=True).then_inc(consts, 1)

            def w_low(blk):
                pool.wait_ge(wh_ready, blk + 1)
                pool.tensor_tensor(w_of(blk, 1)[:, :, :], raw_w[:, blk % 2], w_of(blk, 0)[:, :, :].bitcast(F32),
                                   ALU.subtract).then_inc(w_ready, 1)

            w_low(K_)
            w_low(V_)
            w_low(Q_)
            pool.wait_ge(bias_in, 32)
            for i in range(NT):
                pool.wait_ge(xn_ready, i + 1)
                pool.tensor_tensor(x_sb[0:ROWS[i], i, :], x_sb[0:ROWS[i], i, :], bp_bc[0:ROWS[i], :],
                                   ALU.add).then_inc(xb_ready, 1)
            pool.wait_ge(acc_done, NT)
            pool.memset(kvb[:, :, :], 0.0).then_inc(kv_zero, 1)
            pool.memset(ksb[:, :, :], 0.0).then_inc(kv_zero, 1)
            w_low(PROJ_)
            w_low(NEIGH_)
            for g in range(CH * KC):
                c0, c1 = CHUNKS[g // KC]
                pool.wait_ge(yh_ready, g + 1)
                if g == 0:
                    pool.wait_ge(e_reg, 1)
                pool.tensor_tensor(yT[1][:, g % KC, c0:c1], xn[:, g % 2, 0:c1 - c0],
                                   yT[0][:, g % KC, c0:c1].bitcast(F32), ALU.subtract).then_inc(yl_ready, 1)
            w_low(SELF_)
            pool.wait_ge(w_used, 6)
            pool.iota(iota[:, :], pattern=[[1, SRC_W]], base=0, channel_multiplier=0,
                      allow_small_or_imprecise_dtypes=True).then_inc(gnn_const, 1)
            pool.memset(zero16[:, :], 0.0).then_inc(gnn_const, 1)
            pool.memset(ones16[:, :], 1.0).then_inc(gnn_const, 1)

            def quant_diff(u):
                pool.wait_ge(qa_ready, u + 1)
                if u >= 2:
                    pool.wait_ge(ft_done, u - 1)
                pool.tensor_tensor(q_f[:, u % 2], q_f[:, u % 2], raw_f[:, u % 3], ALU.subtract).then_inc(q_ready, 1)

            for u in range(LEAD):
                quant_diff(u)
            for j in range(FT):
                for c, (c0, c1) in enumerate(CHUNKS):
                    if c < 2:
                        quant_diff(2 * j + c + LEAD)
                    g = j * CH + c
                    pool.wait_ge(hh_ready, g + 1)
                    pool.tensor_tensor(hT[1][:, j, c0:c1], act_f[:, g % 3, 0:c1 - c0],
                                       hT[0][:, j, c0:c1].bitcast(F32), ALU.subtract).then_inc(hl_ready, 1)
            for u in range(2 * FT + LEAD, UNITS_W):
                quant_diff(u)

        @block.scalar
        def _(act):
            def w_high(blk):
                act.wait_ge(raw_in[blk % 2], 16 * (blk // 2 + 1))
                if blk >= 3:
                    act.wait_ge(w_used, blk - 2)
                act.activation(w_of(blk, 0)[:, :, :], raw_w[:, blk % 2], ACT.Copy).then_inc(wh_ready, 1)

            act.wait_ge(eps_set, 1)
            for g, (i0, i1) in enumerate([(0, 2), (2, NT)]):
                act.wait_ge(stat_done, g + 1)
                act.activation(rstd[:, i0:i1], mv[:, i0:i1, 1], ACT.Sqrt, bias=eps_c[:, 0:1]).then_inc(std_done, 1)
                if g == 0:
                    w_high(K_)
                    w_high(V_)

            def k_exp(i):
                r = ROWS[i]
                act.wait_ge(k_done, i + 1)
                if i >= 2:
                    act.wait_ge(kf_ready, i - 1)
                act.activation(ex[0:r, i % 2], ps[0:r, K_BANK + i % 2, :], ACT.Exp).then_inc(ek_ready, 1)

            def v_copy(i):
                r = ROWS[i]
                act.wait_ge(v_done, i + 1)
                if i == 0:
                    act.wait_ge(consts, 2)
                if i >= 2:
                    act.wait_ge(acc_done, i - 1)
                act.activation(vx[0:r, i % 2, :, 0:P],
                               ps[0:r, V_BANK + i % 2, :].rearrange("p (h n) -> p h n", h=KC),
                               ACT.Copy).then_inc(v_ready, 1)

            for s in range(NT + 2):
                if s < NT:
                    act.wait_ge(t_done, s + 1)
                    act.activation(xnT[0][:, :, cols(s)], ps[:, T_BANK + s % 2, :].rearrange(
                        "p (k n) -> p k n", k=KC)[:, :, 0:ROWS[s]], ACT.Copy).then_inc(th_ready, 1)
                if s == 2:
                    w_high(Q_)
                if s >= 2:
                    k_exp(s - 2)
                    v_copy(s - 2)
            w_high(PROJ_)
            w_high(NEIGH_)
            for s in range(CH * KC + 3):
                if s < CH * KC:
                    c0, c1 = CHUNKS[s // KC]
                    act.wait_ge(q_done, s + 1)
                    if s >= 2:
                        act.wait_ge(qf_ready, s - 1)
                    act.activation(ex[:, s % 2, 0:c1 - c0], ps[:, K_BANK + s % 2, 0:c1 - c0],
                                   ACT.Exp).then_inc(ek_ready, 1)
                if s == CH * KC:
                    w_high(SELF_)
                if s >= 3:
                    g = s - 3
                    c0, c1 = CHUNKS[g // KC]
                    act.wait_ge(y_ready, g + 1)
                    act.activation(yT[0][:, g % KC, c0:c1], xn[:, g % 2, 0:c1 - c0], ACT.Copy).then_inc(yh_ready, 1)
            for i in range(NT):
                r = ROWS[i]
                act.wait_ge(p_done, i + 1)
                act.activation(pn[0][0:r, i, :], ps[0:r, V_BANK + i % 2, :], ACT.Copy).then_inc(ph_ready, 1)

            def counts_high(d):
                act.wait_ge(a_done, d + 1)
                if d >= 2:
                    act.wait_ge(msg_done, d - 1)
                act.activation(cnt[d % 2][0][:, :, :], counts_ps(SRC_W).rearrange("p (k n) -> p k n", k=NT),
                               ACT.Copy).then_inc(ah_ready, 1)

            def norm_parts(d):
                r = ROWS[d]
                act.wait_ge(h_ready, d + 1)
                act.activation(ex[0:r, d % 2], kf[0:r, d % 2], ACT.Square, accum_out=col[0:r, d % 2:d % 2 + 1]
                               ).then_inc(act_step, 1)
                act.wait_ge(act_step, d + 1)
                act.activation(col[0:r, 2 + d % 2:3 + d % 2], col[0:r, d % 2:d % 2 + 1], ACT.Sqrt).then_inc(ss_ready, 1)
                act.wait_ge(st2_ready, d + 1)
                act.activation(col[0:r, 4 + d % 2:5 + d % 2], mv2[0:r, d % 2, 1:2], ACT.Sqrt, bias=eps_c[0:r, 0:1]
                               ).then_inc(sd2_ready, 1)

            def t2_high(d):
                act.wait_ge(t2_done, d + 1)
                act.activation(xnT[0][:, :, cols(d)], ps[:, T_BANK + d % 2, :].rearrange(
                    "p (k n) -> p k n", k=KC)[:, :, 0:ROWS[d]], ACT.Copy).then_inc(t2h_ready, 1)

            for s in range(NT + 3):
                if s < NT:
                    counts_high(s)
                if s >= 3:
                    t2_high(s - 3)
                if 2 <= s < NT + 2:
                    norm_parts(s - 2)

            def weight_high(u):
                act.wait_ge(ft_done, u + 1)
                if u < 2 * FT and u >= 4:
                    act.wait_ge(gu_done, 2 * CH * ((u - 4) // 2) + 2 * CH)
                if u == 2 * FT:
                    act.wait_ge(ffn1_done, 1)
                act.activation(ffn_weight_T(u, 0), ps[:, T_BANK + u % 2, :].rearrange("p (k n) -> p k n", k=KC),
                               ACT.Copy).then_inc(fh_ready, 1)

            for u in range(LEAD):
                weight_high(u)
            for j in range(FT):
                for c, (c0, c1) in enumerate(CHUNKS):
                    g = j * CH + c
                    w = c1 - c0
                    act.wait_ge(gu_done, 2 * g + 1)
                    if g >= 3:
                        act.wait_ge(hl_ready, g - 2)
                    act.activation(act_f[:, g % 3, 0:w], ps[:, PE_GU + c, 0:w], ACT.Silu).then_inc(silu_ready, 1)
                    act.wait_ge(hid_ready, g + 1)
                    act.activation(hT[0][:, j, c0:c1], act_f[:, g % 3, 0:w], ACT.Copy).then_inc(hh_ready, 1)
                    if c < 2 and 2 * j + c + LEAD < 2 * FT:
                        weight_high(2 * j + c + LEAD)
            for u in range(2 * FT, UNITS_W):
                weight_high(u)

        @block.vector
        def _(dve):
            steps = [0]

            def step(ins):
                steps[0] += 1
                ins.then_inc(dve_step, 1)
                dve.wait_ge(dve_step, steps[0])

            step(dve.memset(mv[:, :, :], 1.0))
            dve.memset(eps_c[:, :], LN_EPS).then_inc(eps_set, 1)
            for g, (i0, i1) in enumerate(X_LOADS):
                dve.wait_ge(x_in[g], 16)
                for i in range(i0, i1):
                    r = ROWS[i]
                    step(dve.bn_stats(stats[0:r, i % 2, :], x_sb[0:r, i, :]))
                    last = dve.bn_aggr(mv[0:r, i, :], stats[0:r, i % 2, :])
                    if i in (1, NT - 1):
                        last.then_inc(stat_done, 1)

            def layer_norm(i):
                r = ROWS[i]
                if i >= 2:
                    dve.wait_ge(t_done, i - 1)
                dve.tensor_scalar(xn[0:r, i % 2], x_sb[0:r, i, :], mv[0:r, i, 0:1], rstd[0:r, i:i + 1],
                                  ALU.subtract, ALU.mult).then_inc(xn_ready, 1)

            def k_feature(i):
                r = ROWS[i]
                dve.wait_ge(ek_ready, i + 1)
                step(dve.tensor_scalar(ex[0:r, i % 2], ex[0:r, i % 2], 1.0, None, ALU.min))
                if i >= 2:
                    dve.wait_ge(acc_done, i - 1)
                dve.scalar_tensor_tensor(out=kf[0:r, i % 2], in0=ps[0:r, K_BANK + i % 2, :], scalar=0.0,
                                         in1=ex[0:r, i % 2], op0=ALU.max, op1=ALU.add).then_inc(kf_ready, 1)

            def low_T(i, high_done, ready):
                dve.wait_ge(high_done, i + 1)
                dve.tensor_tensor(xnT[1][:, :, cols(i)], ps[:, T_BANK + i % 2, :].rearrange(
                    "p (k n) -> p k n", k=KC)[:, :, 0:ROWS[i]], xnT[0][:, :, cols(i)].bitcast(F32),
                    ALU.subtract).then_inc(ready, 1)

            dve.wait_ge(std_done, 1)
            step(dve.reciprocal(rstd[:, 0:2], rstd[:, 0:2]))
            layer_norm(0)
            layer_norm(1)
            dve.wait_ge(std_done, 2)
            step(dve.reciprocal(rstd[:, 2:NT], rstd[:, 2:NT]))
            for s in range(NT + 2):
                if s < NT:
                    low_T(s, th_ready, xnT_ready)
                if s + 2 < NT:
                    layer_norm(s + 2)
                if s >= 2:
                    k_feature(s - 2)

            dve.wait_ge(edge_in, 32)
            step(dve.tensor_copy(edge_f[:, :, :], edge_i[:, :, :]))
            dve.tensor_reduce(rng[:, 0:1], edge_f[:, 1, :], AX_X, ALU.min)
            dve.tensor_reduce(rng[:, 1:2], edge_f[:, 1, :], AX_X, ALU.max).then_inc(e_f32, 1)
            dve.wait_ge(acc_done, NT)
            dve.wait_ge(kv_zero, 2)
            acc = ps[:, ACC_BANK:ACC_BANK + 2, :].rearrange("p b (h n) -> p b h n", h=2)
            for h in range(2):
                part = slice(HEAD * h, HEAD * h + HEAD)
                dve.tensor_copy(kvb[part, :, part].rearrange("p (b h) n -> p b h n", b=2), acc[part, :, :, part])
                dve.tensor_copy(ksb[part, :, part].rearrange("p (b h) n -> p b h n", b=2),
                                acc[part, :, :, P:P + 1].to_broadcast([HEAD, 2, 2, HEAD])).then_inc(kvb_ready, 1)
            dve.wait_ge(e_t, 1)
            dve.tensor_copy(edge[0:UK, :, :, :].rearrange("p a k m -> p (a k m)"),
                            ps[0:UK, V_BANK, 0:4 * UNITS]).then_inc(e_copied, 1)

            dve.wait_ge(e_bc, 1)
            dve.wait_ge(consts, 6)
            lowest, highest = ps[0:NT, V_BANK + 1, 0:UNITS], ps[0:NT, V_BANK + 1, UNITS:2 * UNITS]
            step(dve.tensor_scalar(wcol[:, 0:1], thr[:, :], float(P), None, ALU.add))
            step(dve.tensor_scalar(win[:, 0, :], highest, thr[:, 0:1], None, ALU.is_ge))
            step(dve.scalar_tensor_tensor(out=win[:, 1, :], in0=lowest, scalar=wcol[:, 0:1], in1=win[:, 0, :],
                                          op0=ALU.is_lt, op1=ALU.mult))
            step(dve.tensor_tensor(win[:, 2, :], win[:, 1, :], unit_m[:, 0, :], ALU.mult))
            step(dve.tensor_tensor(win[:, 3, :], win[:, 1, :], unit_m[:, 1, :], ALU.mult))
            step(dve.tensor_reduce(wcol[:, 1:2], win[:, 2, :], AX_X, ALU.min))
            step(dve.tensor_reduce(wcol[:, 2:3], win[:, 3, :], AX_X, ALU.max))
            step(dve.tensor_scalar(wcol[:, 3:4], wcol[:, 1:2], BIG, float(UNITS - 1), ALU.add, ALU.min))
            step(dve.tensor_tensor(wcol[:, 4:5], wcol[:, 2:3], wcol[:, 3:4], ALU.subtract))
            dve.tensor_scalar(wcol[:, 5:6], wcol[:, 4:5], 1.0, None, ALU.max).then_inc(e_win, 1)

            def windows_out():
                dve.wait_ge(e_row, 1)
                step(dve.tensor_copy(wrow[0:1, :, :], ps[0:1, V_BANK, 0:32].rearrange("p (a n) -> p a n", a=2)))
                dve.tensor_copy(wreg[0:1, 0, 0:NT + 1], wrow[0:1, 0, 0:NT + 1])
                dve.tensor_tensor(wreg[0:1, 1, 0:NT], wrow[0:1, 1, 0:NT], wrow[0:1, 0, 0:NT],
                                  ALU.subtract).then_inc(e_reg, 1)

            windows_out()

            def q_feature(g):
                c0, c1 = CHUNKS[g // KC]
                w = c1 - c0
                dve.wait_ge(ek_ready, NT + g + 1)
                step(dve.tensor_scalar(ex[:, g % 2, 0:w], ex[:, g % 2, 0:w], 1.0, None, ALU.min))
                dve.scalar_tensor_tensor(out=qfT[:, g % KC, c0:c1], in0=ps[:, K_BANK + g % 2, 0:w], scalar=0.0,
                                         in1=ex[:, g % 2, 0:w], op0=ALU.max, op1=ALU.add).then_inc(qf_ready, 1)

            def divide(g):
                c0, c1 = CHUNKS[g // KC]
                w = c1 - c0
                dve.wait_ge(nz_done, g + 1)
                step(dve.tensor_scalar(kf[:, g % 2, 0:w], ps[:, T_BANK + g % 2, 0:w], Z_EPS, None, ALU.add))
                step(dve.reciprocal(kf[:, g % 2, 0:w], kf[:, g % 2, 0:w]))
                if g >= 2:
                    dve.wait_ge(yl_ready, g - 1)
                dve.tensor_tensor(xn[:, g % 2, 0:w], ps[:, V_BANK + g % 2, 0:w], kf[:, g % 2, 0:w],
                                  ALU.mult).then_inc(y_ready, 1)

            for s in range(CH * KC + 2):
                if s < CH * KC:
                    q_feature(s)
                if s >= 2:
                    divide(s - 2)

            dve.wait_ge(xb_ready, NT)
            for i in range(NT):
                r = ROWS[i]
                dve.wait_ge(mix_done, i + 1)
                dve.tensor_tensor(x_sb[0:r, i, :], ps[0:r, K_BANK + i % 2, :], x_sb[0:r, i, :],
                                  ALU.add).then_inc(mix_added, 1)
            for i in range(NT):
                r = ROWS[i]
                dve.wait_ge(ph_ready, i + 1)
                dve.tensor_tensor(pn[1][0:r, i, :], ps[0:r, V_BANK + i % 2, :], pn[0][0:r, i, :].bitcast(F32),
                                  ALU.subtract).then_inc(p_ready, 1)
                dve.wait_ge(s_done, i + 1)
                dve.tensor_tensor(self_sb[0:r, i, :], ps[0:r, T_BANK + i % 2, :], b_bc[0:r, :],
                                  ALU.add).then_inc(s_ready, 1)

            dve.wait_ge(gnn_const, 3)

            def one_hots(d):
                first = dve.value_load(wreg[0:1, 0, d:d + 1], min_val=0, max_val=UNITS * NT)
                last = dve.value_load(wreg[0:1, 0, d + 1:d + 2], min_val=1, max_val=UNITS * NT)
                offset = dve.value_load(wreg[0:1, 1, d:d + 1], min_val=-UNITS * NT, max_val=UNITS)
                with dve.Fori(first, last) as i:
                    m = nc.s_assert_within(i + offset, 0, UNITS - 1, skip_runtime_bounds_check_because=
                                           "a window's first unit is at least 0 and its last at most the last unit")
                    for k in range(2):
                        dve.wait_ge(hot_free, i * 2 + (k + 1))
                        dve.tensor_scalar(src_hot[0:UK, k, :], iota[0:UK, :], edge[0:UK, 0, k, bass.ds(m, 1)],
                                          None, ALU.is_equal)
                        dve.tensor_scalar(dst_hot[0:UK, k, :], iota[0:UK, d * P:(d + 1) * P],
                                          edge[0:UK, 1, k, bass.ds(m, 1)], None,
                                          ALU.is_equal).then_inc(hot_ready, 1)

            def counts_low(d):
                dve.wait_ge(ah_ready, d + 1)
                step(dve.tensor_scalar(col[:, 6:7], counts_ps(DEG + 1)[:, DEG:DEG + 1], 1.0, None, ALU.max))
                dve.reciprocal(rdeg[:, d:d + 1], col[:, 6:7])
                dve.tensor_tensor(cnt[d % 2][1][:, :, :], counts_ps(SRC_W).rearrange("p (k n) -> p k n", k=NT),
                                  cnt[d % 2][0][:, :, :].bitcast(F32), ALU.subtract).then_inc(a_ready, 1)

            def node_update(d):
                r = ROWS[d]
                s = d % 2
                dve.wait_ge(msg_done, d + 1)
                step(dve.scalar_tensor_tensor(out=kf[0:r, s], in0=ps[0:r, MSG_BANK + s, :], scalar=rdeg[0:r, d:d + 1],
                                              in1=self_sb[0:r, d, :], op0=ALU.mult, op1=ALU.add))
                dve.scalar_tensor_tensor(out=kf[0:r, s], in0=kf[0:r, s], scalar=SLOPE, in1=kf[0:r, s],
                                         op0=ALU.mult, op1=ALU.max).then_inc(h_ready, 1)
                dve.wait_ge(h_ready, d + 1)
                dve.wait_ge(ss_ready, d + 1)
                step(dve.tensor_scalar(col[0:r, 8:9], col[0:r, 2 + s:3 + s], NORM_EPS, None, ALU.max))
                step(dve.reciprocal(col[0:r, 9:10], col[0:r, 8:9]))
                step(dve.scalar_tensor_tensor(out=x_sb[0:r, d, :], in0=kf[0:r, s], scalar=col[0:r, 9:10],
                                              in1=x_sb[0:r, d, :], op0=ALU.mult, op1=ALU.add))
                step(dve.bn_stats(stats[0:r, s, :], x_sb[0:r, d, :]))
                dve.bn_aggr(mv2[0:r, s, :], stats[0:r, s, :]).then_inc(st2_ready, 1)
                dve.wait_ge(st2_ready, d + 1)
                dve.wait_ge(sd2_ready, d + 1)
                step(dve.reciprocal(col[0:r, 10:11], col[0:r, 4 + s:5 + s]))
                if d >= 2:
                    dve.wait_ge(t2_done, d - 1)
                dve.tensor_scalar(xn[0:r, s], x_sb[0:r, d, :], mv2[0:r, s, 0:1], col[0:r, 10:11],
                                  ALU.subtract, ALU.mult).then_inc(xn2_ready, 1)

            for s in range(NT + 3):
                if s < NT:
                    one_hots(s)
                    counts_low(s)
                if s >= 3:
                    low_T(s - 3, t2h_ready, xn2T_ready)
                if 2 <= s < NT + 2:
                    node_update(s - 2)

            def quantize(u):
                s = u % 3
                m = u % 2
                dve.wait_ge(f_in[s], 16 * (u // 3 + 1))
                step(dve.tensor_reduce(scal[:, m, 0, :], raw_f[:, s], AX_X, ALU.add, apply_absolute_value=True))
                step(dve.tensor_scalar(scal[:, m, 0, :], scal[:, m, 0, :], 1.0 / P, Q_EPS, ALU.mult, ALU.add))
                dve.tensor_scalar(scal[:, m, 1, :], scal[:, m, 0, :], 0.5, None, ALU.mult)
                step(dve.tensor_scalar(scal[:, m, 2, :], scal[:, m, 0, :], -0.5, None, ALU.mult))
                if u >= 2:
                    dve.wait_ge(ft_done, u - 1)
                for c in range(KC):
                    dve.tensor_scalar(q_f[:, m, c, :], raw_f[:, s, c, :], scal[:, m, 1, c:c + 1],
                                      scal[:, m, 0, c:c + 1], ALU.is_gt, ALU.mult)
                for c in range(KC):
                    last = dve.tensor_scalar(raw_f[:, s, c, :], raw_f[:, s, c, :], scal[:, m, 2, c:c + 1],
                                             scal[:, m, 0, c:c + 1], ALU.is_lt, ALU.mult)
                last.then_inc(qa_ready, 1)

            def weight_low(u):
                dve.wait_ge(fh_ready, u + 1)
                dve.tensor_tensor(ffn_weight_T(u, 1), ps[:, T_BANK + u % 2, :].rearrange("p (k n) -> p k n", k=KC),
                                  ffn_weight_T(u, 0).bitcast(F32), ALU.subtract).then_inc(fw_ready, 1)

            for u in range(LEAD):
                quantize(u)
            for u in range(LEAD):
                weight_low(u)
                quantize(u + LEAD) if u + LEAD < UNITS_W else None
            for j in range(FT):
                for c, (c0, c1) in enumerate(CHUNKS):
                    g = j * CH + c
                    w = c1 - c0
                    dve.wait_ge(gu_done, 2 * g + 2)
                    dve.wait_ge(silu_ready, g + 1)
                    dve.tensor_tensor(act_f[:, g % 3, 0:w], ps[:, PE_GU + CH + c, 0:w], act_f[:, g % 3, 0:w],
                                      ALU.mult).then_inc(hid_ready, 1)
                    u = 2 * j + c + LEAD
                    if c < 2 and u < 2 * FT:
                        weight_low(u)
                        quantize(u + LEAD)
            for u in range(2 * FT, UNITS_W):
                weight_low(u)
                if u + LEAD < UNITS_W:
                    quantize(u + LEAD)
            for i in range(NT):
                r = ROWS[i]
                bank = PE_GU + i % DOWN_A
                dve.wait_ge(down_done, i + 1)
                dve.tensor_tensor(x_sb[0:r, i, :], ps[0:r, bank, :], x_sb[0:r, i, :], ALU.add).then_inc(y_final, 1)

        @block.tensor
        def _(pe):
            def transposes(i, source, bank):
                r = ROWS[i]
                for k in range(KC):
                    last = pe.transpose(ps[:, bank, k * P:k * P + r], source[0:r, k * P:(k + 1) * P], ident[0:r, 0:r])
                return last

            def product(out_, pairs):
                n = 0
                for lhs, rhs in pairs:
                    for ql, qr in PASSES:
                        last = pe.matmul(out_, lhs(ql), rhs(qr), start=(n == 0), stop=(n == 3 * len(pairs) - 1))
                        n += 1
                return last

            def node_rows(i, blk, bank, left=xnT):
                return product(ps[0:ROWS[i], bank, :],
                               [(lambda q, k=k: left[q][:, k, cols(i)], lambda q, k=k: w_of(blk, q)[:, k, :])
                                for k in range(KC)])

            def kv_accumulate(i):
                r = ROWS[i]
                pe.wait_ge(kf_ready, i + 1)
                pe.wait_ge(v_ready, i + 1)
                for pr in range(KC):
                    last = pe.matmul(ps[:, ACC_BANK + pr // 2, 256 * (pr % 2):256 * (pr % 2) + P + 2],
                                     kf[0:r, i % 2, pr * P:(pr + 1) * P], vx[0:r, i % 2, pr, :],
                                     start=(i == 0 and pr % 2 == 0), stop=(i == NT - 1 and pr % 2 == 1), skip_group_check=True)
                last.then_inc(acc_done, 1)

            pe.wait_ge(consts, 1)
            for s in range(NT + 3):
                if s < NT:
                    pe.wait_ge(xn_ready, s + 1)
                    if s >= 2:
                        pe.wait_ge(xnT_ready, s - 1)
                    transposes(s, xn[:, s % 2, :], T_BANK + s % 2).then_inc(t_done, 1)
                if 2 <= s < NT + 2:
                    i = s - 2
                    pe.wait_ge(xnT_ready, i + 1)
                    if i == 0:
                        pe.wait_ge(w_ready, 2)
                    if i >= 2:
                        pe.wait_ge(kf_ready, i - 1)
                    node_rows(i, K_, K_BANK + i % 2).then_inc(k_done, 1)
                    if i >= 2:
                        pe.wait_ge(v_ready, i - 1)
                    last = node_rows(i, V_, V_BANK + i % 2)
                    last.then_inc(v_done, 1)
                if s >= 3:
                    kv_accumulate(s - 3)
            pe.wait_ge(v_done, NT)
            pe.sem_inc(w_used, 2)

            pe.wait_ge(v_ready, NT)
            pe.wait_ge(e_f32, 1)
            for a in range(2):
                for k in range(2):
                    at_ = (2 * a + k) * UNITS
                    last = pe.transpose(ps[0:UK, V_BANK, at_:at_ + UNITS], edge_f[:, a, k * UK:(k + 1) * UK],
                                        ident[0:UNITS, 0:UNITS])
            last.then_inc(e_t, 1)
            for k in range(2):
                last = pe.matmul(ps[0:NT, V_BANK + 1, k * UNITS:(k + 1) * UNITS],
                                 rng[:, k:k + 1].to_broadcast([UNITS, NT]), ident[0:UNITS, 0:UNITS],
                                 start=(k == 0), stop=(k == 1), skip_group_check=True)
            last.then_inc(e_bc, 1)

            def window_rows():
                pe.wait_ge(e_win, 1)
                pe.wait_ge(e_copied, 1)
                pe.matmul(ps[0:1, V_BANK, 0:NT + 1], wcol[:, 5:6], prefix[:, :], start=True, stop=False,
                          skip_group_check=True)
                pe.matmul(ps[0:1, V_BANK, 16:16 + NT], wcol[:, 3:4], ident[0:NT, 0:NT], start=False, stop=True,
                          skip_group_check=True).then_inc(e_row, 1)

            def q_rows(g):
                c0, c1 = CHUNKS[g // KC]
                c = g % KC
                if g >= 2:
                    pe.wait_ge(qf_ready, g - 1)
                product(ps[:, K_BANK + g % 2, 0:c1 - c0],
                        [(lambda q, k=k: w_of(Q_, q)[:, k, c * P:(c + 1) * P], lambda q, k=k: xnT[q][:, k, c0:c1])
                         for k in range(KC)]).then_inc(q_done, 1)

            def attend(g):
                c0, c1 = CHUNKS[g // KC]
                pe.wait_ge(qf_ready, g + 1)
                if g == 0:
                    pe.wait_ge(kvb_ready, 2)
                    pe.wait_ge(e_reg, 1)
                if g >= 2:
                    pe.wait_ge(y_ready, g - 1)
                pe.matmul(ps[:, V_BANK + g % 2, 0:c1 - c0], kvb[:, g % KC, :], qfT[:, g % KC, c0:c1], start=True, stop=True)
                pe.matmul(ps[:, T_BANK + g % 2, 0:c1 - c0], ksb[:, g % KC, :], qfT[:, g % KC, c0:c1],
                          start=True, stop=True).then_inc(nz_done, 1)

            pe.wait_ge(w_ready, Q_ + 1)
            for s in range(CH * KC + 3):
                if s < CH * KC:
                    q_rows(s)
                if s == 1:
                    window_rows()
                if s >= 3:
                    attend(s - 3)
            pe.wait_ge(q_done, CH * KC)
            pe.sem_inc(w_used, 1)

            pe.wait_ge(w_ready, PROJ_ + 1)
            for i in range(NT):
                pe.wait_ge(yl_ready, KC * (i // TILES_PER_CHUNK + 1))
                if i < 2:
                    pe.wait_ge(qf_ready, CH * KC)
                else:
                    pe.wait_ge(mix_added, i - 1)
                node_rows(i, PROJ_, K_BANK + i % 2, yT).then_inc(mix_done, 1)
            pe.wait_ge(mix_done, NT)
            pe.sem_inc(w_used, 1)
            pe.wait_ge(w_ready, SELF_ + 1)
            pe.wait_ge(y_ready, CH * KC)
            for i in range(NT):
                if i >= 2:
                    pe.wait_ge(p_ready, i - 1)
                    pe.wait_ge(s_ready, i - 1)
                node_rows(i, NEIGH_, V_BANK + i % 2).then_inc(p_done, 1)
                node_rows(i, SELF_, T_BANK + i % 2).then_inc(s_done, 1)
            pe.wait_ge(s_done, NT)
            pe.sem_inc(w_used, 2)

            def count_edges(d):
                if d == 0:
                    pe.wait_ge(gnn_const, 3)
                    pe.wait_ge(p_ready, NT)
                    pe.sem_inc(hot_free, 2)
                else:
                    pe.wait_ge(a_ready, d)
                for bank in range(3):
                    pe.matmul(ps[:, A_BANK + bank, :], zero16[:, 0:P], zero16[:, :], start=True, stop=False,
                              skip_group_check=True)
                first = pe.value_load(wreg[0:1, 0, d:d + 1], min_val=0, max_val=UNITS * NT)
                last_ = pe.value_load(wreg[0:1, 0, d + 1:d + 2], min_val=1, max_val=UNITS * NT)
                with pe.Fori(first, last_) as i:
                    for k in range(2):
                        pe.wait_ge(hot_ready, i * 2 + (k + 1))
                        for s in range(NT):
                            pe.matmul(counts_ps(SRC_W)[:, s * P:(s + 1) * P], src_hot[0:UK, k, s * P:(s + 1) * P],
                                      dst_hot[0:UK, k, :], start=False, stop=False, skip_group_check=True)
                        pe.matmul(counts_ps(DEG + 1)[:, DEG:DEG + 1], dst_hot[0:UK, k, :], ones16[0:UK, 0:1],
                                  start=False, stop=False, skip_group_check=True).then_inc(hot_free, 1)
                for bank in range(3):
                    last = pe.matmul(ps[:, A_BANK + bank, 0:2], zero16[:, 0:P], zero16[:, 0:2], start=False, stop=True,
                                     skip_group_check=True)
                last.then_inc(a_done, 1)

            def messages(d):
                pe.wait_ge(a_ready, d + 1)
                if d < 2:
                    pe.wait_ge(mix_added, NT)
                else:
                    pe.wait_ge(h_ready, d - 1)
                product(ps[0:ROWS[d], MSG_BANK + d % 2, :],
                        [(lambda q, s=s: cnt[d % 2][q][0:ROWS[s], s, 0:ROWS[d]], lambda q, s=s: pn[q][0:ROWS[s], s, :])
                         for s in range(NT)]).then_inc(msg_done, 1)

            for s in range(NT + 2):
                if s < NT:
                    count_edges(s)
                if 1 <= s < NT + 1:
                    messages(s - 1)
                if s >= 2:
                    d = s - 2
                    pe.wait_ge(xn2_ready, d + 1)
                    if d < 2:
                        pe.wait_ge(s_ready, NT)
                    else:
                        pe.wait_ge(xn2T_ready, d - 1)
                    transposes(d, xn[:, d % 2, :], T_BANK + d % 2).then_inc(t2_done, 1)

            def weight_T(u):
                pe.wait_ge(q_ready, u + 1)
                if u < 2:
                    pe.wait_ge(xn2T_ready, NT)
                else:
                    pe.wait_ge(fw_ready, u - 1)
                for k in range(KC):
                    last = pe.transpose(ps[:, T_BANK + u % 2, k * P:(k + 1) * P], q_f[:, u % 2, k, :], ident[:, :])
                last.then_inc(ft_done, 1)

            def gate_up(j, c):
                c0, c1 = CHUNKS[c]
                g = j * CH + c
                pe.wait_ge(fw_ready, 2 * j + 2)
                for part in range(2):
                    if part == 0 and j > 0:
                        pe.wait_ge(hid_ready, g - CH + 1)
                    elif part == 0:
                        pe.wait_ge(xn2T_ready, NT)
                        pe.wait_ge(h_ready, NT)
                    last = product(ps[:, PE_GU + part * CH + c, 0:c1 - c0],
                                   [(lambda q, k=k: guT[(2 * j + part) % 4][q][:, k, :],
                                     lambda q, k=k: xnT[q][:, k, c0:c1]) for k in range(KC)])
                    last.then_inc(gu_done, 1)

            for u in range(LEAD):
                weight_T(u)
            for j in range(FT):
                for c in range(CH):
                    gate_up(j, c)
                    if c < 2:
                        weight_T(2 * j + c + LEAD)
            pe.wait_ge(gu_done, 2 * CH * FT)
            pe.sem_inc(ffn1_done, 1)

            def down(i, j):
                for n, (ql, qr) in enumerate(PASSES):
                    last = pe.matmul(ps[0:ROWS[i], PE_GU + i % DOWN_A, :], hT[ql][:, j, cols(i)], wdT[qr][j][:, :],
                                     start=(j == 0 and n == 0), stop=(j == FT - 1 and n == 2))
                if j == FT - 1:
                    last.then_inc(down_done, 1)

            pe.wait_ge(hl_ready, CH * FT)
            for j in range(FT):
                pe.wait_ge(fw_ready, 2 * FT + j + 1)
                for i in range(DOWN_A):
                    down(i, j)
                if 2 * FT + j + LEAD < UNITS_W:
                    weight_T(2 * FT + j + LEAD)
            for i in range(DOWN_A, NT):
                pe.wait_ge(y_final, i - DOWN_A + 1)
                for j in range(FT):
                    down(i, j)


_INS = ['x', 'src', 'dst', 'L0_gnn_W_self', 'L0_gnn_W_neigh', 'L0_gnn_b', 'L0_mix_w_qkv', 'L0_mix_w_proj',
        'L0_mix_b_proj', 'L0_ffn_w_gate', 'L0_ffn_w_up', 'L0_ffn_w_down']


def kernel(**inputs):
    import numpy as _np
    import concourse.bacc as _bacc
    from concourse import mybir as _mybir
    from concourse.bass_utils import run_bass_kernel_spmd as _run

    nc = _bacc.Bacc("TRN2", target_bir_lowering=False, num_devices=1)
    arrays, args = {}, []
    for name in _INS:
        a = _np.ascontiguousarray(inputs[name])
        arrays[f"in_{name}"] = a
        args.append(nc.dram_tensor(f"in_{name}", a.shape, _mybir.dt.from_np(a.dtype), kind="ExternalInput").ap())
    args.append(nc.dram_tensor("out_0", (N, D), _mybir.dt.float32, kind="ExternalOutput").ap())
    gnn_mix_ffn_kernel(nc, *args)
    r = _run(nc, [arrays], core_ids=[0])
    return r.results[0]["out_0"]
```

```python
from contextlib import ExitStack

import concourse.bass as bass
from concourse import mybir

F32 = mybir.dt.float32
F32R = mybir.dt.float32r
F16 = mybir.dt.float16
I32 = mybir.dt.int32
ALU = mybir.AluOpType
ACT = mybir.ActivationFunctionType
AX_X = mybir.AxisListType.X

P = 128
N = 1250
D = 512
KC = D // P
NT = (N + P - 1) // P
ROWS = [min(P, N - i * P) for i in range(NT)]
CHUNKS = [(0, 512), (512, 1024), (1024, N)]
CH = len(CHUNKS)
TILES_PER_CHUNK = 512 // P
HEAD = 64
EDGES = 20000
COLS = 2
UK = 125
UNIT = COLS * UK
RING = 4
UNITS = EDGES // UNIT
SRC_W = NT * P
FFN = 1408
FT = FFN // P
UNITS_W = 3 * FT
LN_EPS = 1e-5
Q_EPS = 1e-5
Z_EPS = 1e-6
NORM_EPS = 1e-12
SLOPE = 0.01
BIG = 999.0

PASSES = [(0, 0), (0, 1), (1, 0)]


def gnn_mix_ffn_kernel(nc, x, src, dst, W_self, W_neigh, b, w_qkv, w_proj, b_proj, w_gate, w_up, w_down, out):
    ctx = ExitStack()
    with ctx:
        arena = 16512

        def at(name, shape, dt, offset):
            return nc.alloc_sbuf_tensor_at(name, shape, dt, offset=arena + offset)

        def sem(name):
            return ctx.enter_context(nc.semaphore(name))

        x_sb = at("x_sb", [P, NT, D], F32, 0)
        XT = 20480
        xnT = [at("xnT_h", [P, KC, N], F32R, XT), at("xnT_l", [P, KC, N], F32R, XT + 20000)]
        wdT = [[None] * FT, [None] * FT]
        WB = 60544
        raw_w = at("raw_w", [P, 2, KC, D], F32, WB)
        WS = WB + 16384
        w_hl = [[at(f"w_{'hl'[q]}{s}", [P, KC, D], F32R, WS + 16384 * s + 8192 * q) for q in (0, 1)] for s in range(3)]
        R1 = WS + 3 * 16384
        yT = [at("yT_h", [P, KC, N], F32R, R1), at("yT_l", [P, KC, N], F32R, R1 + 20000)]
        pn = [at("pn_h", [P, NT, D], F32R, R1), at("pn_l", [P, NT, D], F32R, R1 + 20480)]
        R2 = R1 + 40960
        qfT = at("qfT", [P, KC, N], F32, R2)
        self_sb = at("self_sb", [P, NT, D], F32, R2)
        src_hot = at("src_hot", [P, RING * COLS, SRC_W], F16, WB)
        iota = at("iota", [P, SRC_W], F16, WS + 4096)
        zero16 = at("zero16", [P, 512], F16, WS + 6656)
        dst_hot = at("dst_hot", [P, RING * COLS, P], F16, WS + 7680)
        cnt_sb = at("cnt_sb", [P, SRC_W], F32, WS + 9728)
        junk = at("junk", [P, D], F16, WS + 14848)
        cnt = [at("cnt_h", [P, NT, P], F32R, WS + 16384), at("cnt_l", [P, NT, P], F32R, WS + 21504)]
        hT = [at("hT_h", [P, FT, N], F32R, WB), at("hT_l", [P, FT, N], F32R, WB + 55008)]
        WT = WB + 2 * 55008
        C0 = R2 + 20480
        guT = [[at(f"guT_{'hl'[q]}{s}", [P, KC, P], F32R, WT + 4096 * s + 2048 * q) for q in (0, 1)] for s in range(4)]
        first_at = [[WB + 10240, WB + 12288], [WB + 14336, C0 + 6144]]
        guT0 = [[at(f"guT0_{'hl'[q]}{s}", [P, KC, P], F32R, first_at[s][q]) for q in (0, 1)] for s in (0, 1)]
        for j in range(FT):
            base = C0 + 6144 if j == 0 else XT + 4096 * (j - 1) if j < 10 else WT
            for q in (0, 1):
                wdT[q][j] = at(f"wdT_{'hl'[q]}{j}", [P, D], F32R, base + 2048 * q)
        ex = at("ex", [P, 2, D], F32, C0)
        vx = at("vx", [P, 2, KC, P + 2], F32, C0 + 4096)
        kvb = at("kvb", [P, KC, P + 2], F32, C0 + 4096)
        xn = at("xn", [P, 2, D], F32, C0 + 8256)
        kf = at("kf", [P, 2, D], F32, C0 + 12352)
        C1 = C0 + 16448
        b_bc = at("b_bc", [P, D], F32, C1)
        bp_bc = at("bp_bc", [P, D], F32, C1 + 2048)
        raw_f = at("raw_f", [P, 3, KC, P], F32, C0)
        q_f = at("q_f", [P, 2, KC, P], F32, C1)
        edge = at("edge", [P, 2, COLS, UNITS], F32, C1 + 4096)
        ident = at("ident", [P, P], F32, C1 + 5376)
        small = C1 + 5888
        stats = at("stats", [P, 2, 6], F32, small)
        mv = at("mv", [P, NT, 2], F32, small + 64)
        rstd = at("rstd", [P, NT], F32, small + 160)
        mv2 = at("mv2", [P, 2, 2], F32, small + 224)
        col = at("col", [P, 16], F32, small + 256)
        scal = at("scal", [P, 2, 3, KC], F32, small + 320)
        rdeg = at("rdeg", [P, NT], F32, small + 416)
        eps_c = at("eps_c", [P, 1], F32, small + 480)
        rz = at("rz", [P, 2, KC, 2], F32, small + 640)
        act_f = [at(f"act_f{n}", [P, 512], F32, offset)
                 for n, offset in enumerate((C0 + 12352, small + 704, C0 + 10304))]
        E0 = R1 + 20480
        edge_i = at("edge_i", [UNITS, 2, UNIT], I32, E0)
        edge_f = at("edge_f", [UNITS, 2, UNIT], F32, E0 + 2048)
        rng = at("rng", [UNITS, 2], F32, E0 + 4096)
        win = at("win", [NT, 6, UNITS], F32, E0 + 4160)
        wcol = at("wcol", [NT, 8], F32, E0 + 6144)
        prefix = at("prefix", [NT, NT + 1], F32, E0 + 6208)
        unit_m = at("unit_m", [NT, 2, UNITS], F32, E0 + 6272)
        thr = at("thr", [NT, 1], F32, E0 + 6976)
        wrow = at("wrow", [1, 2, 16], F32, E0 + 7008)
        wreg = at("wreg", [1, 2, 16], I32, small + 512)

        ps = ctx.enter_context(nc.psum_tensor("ps", [P, 8, 512], F32))

        x_in = [sem(f"x_in{g}") for g in range(4)]
        raw_in = [sem(f"raw_in{s}") for s in range(2)]
        bias_in = sem("bias_in")
        edge_in = sem("edge_in")
        consts = sem("consts")
        eps_set = sem("eps_set")
        stat_done = sem("stat_done")
        std_done = sem("std_done")
        xn_ready = sem("xn_ready")
        t_done = sem("t_done")
        th_ready = sem("th_ready")
        xnT_ready = sem("xnT_ready")
        wh_ready = sem("wh_ready")
        wk_ready = sem("wk_ready")
        w_ready = sem("w_ready")
        w_used = sem("w_used")
        xb_ready = sem("xb_ready")
        k_done, v_done, acc_done = sem("k_done"), sem("v_done"), sem("acc_done")
        ek_ready = sem("ek_ready")
        kf_ready, v_ready = sem("kf_ready"), sem("v_ready")
        kvb_ready = sem("kvb_ready")
        kv_zero = sem("kv_zero")
        e_f32 = sem("e_f32")
        e_t, e_copied, e_bc, e_win, e_row, e_reg = (sem("e_t"), sem("e_copied"), sem("e_bc"), sem("e_win"),
                                                   sem("e_row"), sem("e_reg"))
        q_done, qf_ready = sem("q_done"), sem("qf_ready")
        att_done, y_ready = sem("att_done"), sem("y_ready")
        yt_done, yh_ready, yl_ready = sem("yt_done"), sem("yh_ready"), sem("yl_ready")
        mix_done, mix_added = sem("mix_done"), sem("mix_added")
        p_done, ph_ready, p_ready = sem("p_done"), sem("ph_ready"), sem("p_ready")
        s_done, s_ready = sem("s_done"), sem("s_ready")
        gnn_const = sem("gnn_const")
        hot_free = sem("hot_free")
        hot_ready = sem("hot_ready")
        a_done = sem("a_done")
        a_copied, deg_ready = sem("a_copied"), sem("deg_ready")
        at_done, ah_ready, a_ready = sem("at_done"), sem("ah_ready"), sem("a_ready")
        msg_done, g_read, h_ready, ss_ready, nrm_ready = (sem("msg_done"), sem("g_read"), sem("h_ready"),
                                                         sem("ss_ready"), sem("nrm_ready"))
        st2_ready, sd2_ready, xn2_ready = sem("st2_ready"), sem("sd2_ready"), sem("xn2_ready")
        t2_done, t2h_ready, xn2T_ready = sem("t2_done"), sem("t2h_ready"), sem("xn2T_ready")
        f_in = [sem(f"f_in{s}") for s in range(3)]
        qa_ready, q_ready = sem("qa_ready"), sem("q_ready")
        ft_done, fh_ready, fw_ready = sem("ft_done"), sem("fh_ready"), sem("fw_ready")
        gu_done, silu_ready, hid_ready, hh_ready, hl_ready = (sem("gu_done"), sem("silu_ready"), sem("hid_ready"),
                                                             sem("hh_ready"), sem("hl_ready"))
        ffn1_done = sem("ffn1_done")
        down_done, y_final = sem("down_done"), sem("y_final")
        out_done = sem("out_done")
        dve_step, act_step, pool_step = sem("dve_step"), sem("act_step"), sem("pool_step")

        LEAD = 2
        X_LOADS = [(0, 2), (2, 6), (6, NT - 1), (NT - 1, NT)]
        STAT_GROUPS = [(0, 2), (2, 6), (6, NT)]
        K_, V_, Q_, PROJ_, NEIGH_, SELF_ = range(6)
        W_BLOCKS = [w_qkv[:, D:2 * D], w_qkv[:, 2 * D:3 * D], w_qkv[:, 0:D], w_proj, W_neigh, W_self]

        def w_of(block, q):
            return w_hl[block % 3][q]

        T_BANK, K_BANK, V_BANK, ACC_BANK = 0, 2, 4, 6
        ATT_BANK = 4
        A_BANK, AT_BANK = 5, 3
        PE_GU = 2

        def cols(i):
            return slice(i * P, i * P + ROWS[i])

        def counts_ps(width):
            return ps[:, A_BANK:A_BANK + 3, :].rearrange("p b n -> p (b n)")[:, 0:width]

        def msg_bank(d):
            return 2 - d % 2

        def next_weight(j, c):
            if j == 0:
                return LEAD + c - 1 if c >= 1 else None
            return 2 * j + c + LEAD if c < 2 else None

        def weight_bank(u):
            return AT_BANK + u if u < LEAD else T_BANK + u % 2

        EARLY_QUANT = (6, 7)
        DEG = N
        AT_GROUPS = [(0, 4), (4, 8), (8, NT)]

        def head_rows(i, width):
            bank = ATT_BANK + 2 * (i % 2)
            return ps[0:ROWS[i], bank:bank + 2, :].rearrange("p b (h n) -> p (b h) n", h=2)[:, :, 0:width]

        def ffn_weight(u):
            if u < 2 * FT:
                w = (w_gate, w_up)[u % 2]
                return w[(u // 2) * P:(u // 2 + 1) * P, :].rearrange("p (k n) -> p k n", k=KC)
            j = u - 2 * FT
            return w_down.rearrange("(c p) f -> p c f", p=P)[:, :, j * P:(j + 1) * P]

        def gu_T(u, q):
            return guT0[u][q] if u < 2 else guT[u % 4][q]

        def ffn_weight_T(u, q):
            if u < 2 * FT:
                return gu_T(u, q)[:, :, :]
            return wdT[q][u - 2 * FT][:, :].rearrange("p (c n) -> p c n", c=KC)

        ATT_LAG, YT_LAG = 5, 7
        MIX_LAG = CH * KC
        def unit_of(i, offset):
            return nc.s_assert_within(i + offset, 0, UNITS - 1, skip_runtime_bounds_check_because=
                                      "a window's first unit is at least 0 and its last at most the last unit")

        def ring_slot(i):
            return nc.s_assert_within((i & (RING - 1)) * COLS, 0, (RING - 1) * COLS, skip_runtime_bounds_check_because=
                                      "the lowest bits of a step count number the ring's units")

        DOWN_A = 6

        block = ctx.enter_context(nc.Block())

        @block.sync
        def _(sp):
            def load_x(g):
                i0, i1 = X_LOADS[g]
                if i1 < NT:
                    sp.dma_start(x_sb[:, i0:i1, :], x[i0 * P:i1 * P, :].rearrange("(i p) n -> p i n", p=P)
                                 ).then_inc(x_in[g], 16)
                else:
                    sp.dma_start(x_sb[0:ROWS[-1], i0, :], x[i0 * P:N, :]).then_inc(x_in[g], 16)

            def load_w(blk):
                sp.dma_start(raw_w[:, blk % 2], W_BLOCKS[blk].rearrange("(k p) n -> p k n", p=P)
                             ).then_inc(raw_in[blk % 2], 16)

            load_x(0)
            load_w(K_)
            load_w(V_)
            for g in range(1, len(X_LOADS)):
                load_x(g)
            sp.dma_start(bp_bc[:, :], b_proj.partition_broadcast(P)).then_inc(bias_in, 16)
            sp.dma_start(b_bc[:, :], b.partition_broadcast(P)).then_inc(bias_in, 16)
            sp.dma_start(edge_i[:, 0, :], src.rearrange("(m e) -> m e", e=UNIT)).then_inc(edge_in, 16)
            sp.dma_start(edge_i[:, 1, :], dst.rearrange("(m e) -> m e", e=UNIT)).then_inc(edge_in, 16)
            for blk in range(2, 6):
                if blk == 2:
                    sp.wait_ge(wk_ready, 1)
                else:
                    sp.wait_ge(w_ready, blk - 2)
                load_w(blk)
            sp.wait_ge(s_done, NT)
            for u in range(UNITS_W):
                if u >= 3:
                    sp.wait_ge(q_ready, u - 2)
                sp.dma_start(raw_f[:, u % 3], ffn_weight(u)).then_inc(f_in[u % 3], 16)
            for i in range(NT):
                sp.wait_ge(y_final, i + 1)
                sp.dma_start(out[i * P:i * P + ROWS[i], :], x_sb[0:ROWS[i], i, :]).then_inc(out_done, 16)
            sp.wait_ge(out_done, 16 * NT)

        @block.gpsimd
        def _(pool):
            steps = [0]

            def step(ins):
                steps[0] += 1
                ins.then_inc(pool_step, 1)
                pool.wait_ge(pool_step, steps[0])

            step(pool.iota(ident[:, :], pattern=[[1, P]], base=0, channel_multiplier=-1,
                           allow_small_or_imprecise_dtypes=True))
            pool.tensor_scalar(ident[:, :], ident[:, :], 0.0, None, ALU.is_equal).then_inc(consts, 1)
            pool.memset(vx[:, :, :, P:P + 2], 1.0).then_inc(consts, 1)
            step(pool.iota(prefix[:, :], pattern=[[1, NT + 1]], base=0, channel_multiplier=-1,
                           allow_small_or_imprecise_dtypes=True))
            pool.tensor_scalar(prefix[:, :], prefix[:, :], 0.0, None, ALU.is_gt).then_inc(consts, 1)
            pool.iota(thr[:, :], pattern=[[0, 1]], base=0, channel_multiplier=P,
                      allow_small_or_imprecise_dtypes=True).then_inc(consts, 1)
            pool.iota(unit_m[:, 0, :], pattern=[[1, UNITS]], base=-int(BIG), channel_multiplier=0,
                      allow_small_or_imprecise_dtypes=True).then_inc(consts, 1)
            pool.iota(unit_m[:, 1, :], pattern=[[1, UNITS]], base=1, channel_multiplier=0,
                      allow_small_or_imprecise_dtypes=True).then_inc(consts, 1)

            def w_low(blk):
                pool.wait_ge(wh_ready, blk + 1)
                pool.tensor_tensor(w_of(blk, 1)[:, :, :], raw_w[:, blk % 2], w_of(blk, 0)[:, :, :].bitcast(F32),
                                   ALU.subtract).then_inc(w_ready, 1)

            w_low(V_)
            w_low(Q_)
            pool.wait_ge(bias_in, 32)
            for i in range(NT):
                pool.wait_ge(xn_ready, i + 1)
                pool.tensor_tensor(x_sb[0:ROWS[i], i, :], x_sb[0:ROWS[i], i, :], bp_bc[0:ROWS[i], :],
                                   ALU.add).then_inc(xb_ready, 1)
            pool.wait_ge(acc_done, NT)
            pool.memset(kvb[:, :, :], 0.0).then_inc(kv_zero, 1)
            w_low(PROJ_)
            w_low(NEIGH_)
            w_low(SELF_)
            pool.wait_ge(w_used, 4)
            pool.iota(iota[:, :], pattern=[[1, SRC_W]], base=0, channel_multiplier=0,
                      allow_small_or_imprecise_dtypes=True).then_inc(gnn_const, 1)
            pool.memset(zero16[:, :], 0.0).then_inc(gnn_const, 1)
            pool.wait_ge(w_ready, SELF_)
            pool.memset(src_hot[:, :, N:SRC_W], 1.0).then_inc(gnn_const, 1)

            def quant_diff(u):
                pool.wait_ge(qa_ready, u + 1)
                if u >= 2:
                    pool.wait_ge(ft_done, u - 1)
                pool.tensor_tensor(q_f[:, u % 2], q_f[:, u % 2], raw_f[:, u % 3], ALU.subtract).then_inc(q_ready, 1)

            for u in range(2 * LEAD):
                quant_diff(u)
            for j in range(FT):
                for c, (c0, c1) in enumerate(CHUNKS):
                    g = j * CH + c
                    pool.wait_ge(hh_ready, g + 1)
                    pool.tensor_tensor(hT[1][:, j, c0:c1], act_f[g % 3][:, 0:c1 - c0],
                                       hT[0][:, j, c0:c1].bitcast(F32), ALU.subtract).then_inc(hl_ready, 1)
                    u = next_weight(j, c)
                    if u is not None and u < 2 * FT:
                        quant_diff(u + LEAD)
            for u in range(2 * FT + LEAD, UNITS_W):
                quant_diff(u)

        @block.scalar
        def _(act):
            def w_high(blk):
                act.wait_ge(raw_in[blk % 2], 16 * (blk // 2 + 1))
                if blk >= 3:
                    act.wait_ge(w_used, blk - 2)
                act.activation(w_of(blk, 0)[:, :, :], raw_w[:, blk % 2], ACT.Copy).then_inc(wh_ready, 1)

            def std(g):
                i0, i1 = STAT_GROUPS[g]
                act.wait_ge(stat_done, g + 1)
                act.activation(rstd[:, i0:i1], mv[:, i0:i1, 1], ACT.Sqrt, bias=eps_c[:, 0:1]).then_inc(std_done, 1)

            def high_T(i, done, dest, ready):
                act.wait_ge(done, i + 1)
                act.activation(dest[0][:, :, cols(i)], ps[:, T_BANK + i % 2, :].rearrange(
                    "p (k n) -> p k n", k=KC)[:, :, 0:ROWS[i]], ACT.Copy).then_inc(ready, 1)

            def k_exp(i):
                r = ROWS[i]
                act.wait_ge(k_done, i + 1)
                if i >= 2:
                    act.wait_ge(kf_ready, i - 1)
                act.activation(ex[0:r, i % 2], ps[0:r, K_BANK + i % 2, :], ACT.Exp).then_inc(ek_ready, 1)

            def v_copy(i):
                r = ROWS[i]
                act.wait_ge(v_done, i + 1)
                if i == 0:
                    act.wait_ge(consts, 2)
                if i >= 2:
                    act.wait_ge(acc_done, i - 1)
                act.activation(vx[0:r, i % 2, :, 0:P],
                               ps[0:r, V_BANK + i % 2, :].rearrange("p (h n) -> p h n", h=KC),
                               ACT.Copy).then_inc(v_ready, 1)

            act.wait_ge(eps_set, 1)
            std(0)
            w_high(K_)
            w_high(V_)
            high_T(0, t_done, xnT, th_ready)
            high_T(1, t_done, xnT, th_ready)
            std(1)
            std(2)
            for s in range(2, NT + 2):
                if s < NT:
                    high_T(s, t_done, xnT, th_ready)
                if s == 4:
                    w_high(Q_)
                k_exp(s - 2)
                v_copy(s - 2)
            w_high(PROJ_)
            w_high(NEIGH_)
            for s in range(NT + YT_LAG):
                if s < CH * KC:
                    c0, c1 = CHUNKS[s // KC]
                    act.wait_ge(q_done, s + 1)
                    if s >= 2:
                        act.wait_ge(qf_ready, s - 1)
                    act.activation(ex[:, s % 2, 0:c1 - c0], ps[:, K_BANK + s % 2, 0:c1 - c0],
                                   ACT.Exp).then_inc(ek_ready, 1)
                if s == CH * KC:
                    w_high(SELF_)
                if s >= YT_LAG:
                    high_T(s - YT_LAG, yt_done, yT, yh_ready)
            for i in range(NT):
                r = ROWS[i]
                act.wait_ge(p_done, i + 1)
                act.activation(pn[0][0:r, i, :], ps[0:r, V_BANK + i % 2, :], ACT.Copy).then_inc(ph_ready, 1)

            def counts_copy(d):
                act.wait_ge(a_done, d + 1)
                if d >= 1:
                    act.wait_ge(at_done, 3 * d)
                    act.wait_ge(deg_ready, d)
                act.activation(cnt_sb[:, 0:DEG + 1], counts_ps(DEG + 1), ACT.Copy).then_inc(a_copied, 1)

            def counts_high(d, n):
                b0, b1 = AT_GROUPS[n]
                act.wait_ge(at_done, 3 * d + n + 1)
                act.activation(cnt[0][:, b0:b1, :], ps[:, AT_BANK + (3 * d + n) % 2, 0:(b1 - b0) * P].rearrange(
                    "p (k n) -> p k n", k=b1 - b0), ACT.Copy).then_inc(ah_ready, 1)

            def normed_high_T(d):
                act.wait_ge(t2_done, d + 1)
                act.activation(xnT[0][:, :, cols(d)], ps[:, T_BANK, :].rearrange(
                    "p (k n) -> p k n", k=KC)[:, :, 0:ROWS[d]], ACT.Copy).then_inc(t2h_ready, 1)

            def norm_of(d):
                r = ROWS[d]
                act.wait_ge(h_ready, d + 1)
                act.activation(junk[0:r, :], kf[0:r, d % 2], ACT.Square, accum_out=col[0:r, d % 2:d % 2 + 1]
                               ).then_inc(act_step, 1)
                act.wait_ge(act_step, d + 1)
                act.activation(col[0:r, 2 + d % 2:3 + d % 2], col[0:r, d % 2:d % 2 + 1], ACT.Sqrt).then_inc(ss_ready, 1)

            def std2(d):
                r = ROWS[d]
                act.wait_ge(st2_ready, d + 1)
                act.activation(col[0:r, 4 + d % 2:5 + d % 2], mv2[0:r, d % 2, 1:2], ACT.Sqrt, bias=eps_c[0:r, 0:1]
                               ).then_inc(sd2_ready, 1)

            for s in range(NT + 1):
                if s >= 2:
                    norm_of(s - 2)
                if s >= 1:
                    counts_high(s - 1, 2)
                if s < NT:
                    counts_copy(s)
                    counts_high(s, 0)
                    counts_high(s, 1)
                if s >= 2:
                    std2(s - 2)
                if s >= 3:
                    normed_high_T(s - 3)

            def weight_high(u):
                act.wait_ge(ft_done, u + 1)
                if u < 2 * FT and u >= 6:
                    act.wait_ge(gu_done, 2 * CH * ((u - 4) // 2) + 2 * CH)
                if u == 2 * FT + 1:
                    act.wait_ge(ffn1_done, 1)
                act.activation(ffn_weight_T(u, 0), ps[:, weight_bank(u), :].rearrange("p (k n) -> p k n", k=KC),
                               ACT.Copy).then_inc(fh_ready, 1)

            for u in range(LEAD):
                weight_high(u)
            norm_of(NT - 1)
            std2(NT - 1)
            normed_high_T(NT - 2)
            for j in range(FT):
                for c, (c0, c1) in enumerate(CHUNKS):
                    g = j * CH + c
                    w = c1 - c0
                    act.wait_ge(gu_done, 2 * g + 1)
                    if g >= 3:
                        act.wait_ge(hl_ready, g - 2)
                    act.activation(act_f[g % 3][:, 0:w], ps[:, PE_GU + c, 0:w], ACT.Silu).then_inc(silu_ready, 1)
                    act.wait_ge(hid_ready, g + 1)
                    act.activation(hT[0][:, j, c0:c1], act_f[g % 3][:, 0:w], ACT.Copy).then_inc(hh_ready, 1)
                    if g == 0:
                        normed_high_T(NT - 1)
                    u = next_weight(j, c)
                    if u is not None and u < 2 * FT:
                        weight_high(u)
            for u in range(2 * FT, UNITS_W):
                weight_high(u)

        @block.vector
        def _(dve):
            steps = [0]

            def step(ins):
                steps[0] += 1
                ins.then_inc(dve_step, 1)
                dve.wait_ge(dve_step, steps[0])

            step(dve.memset(mv[:, :, :], 1.0))
            dve.memset(eps_c[:, :], LN_EPS).then_inc(eps_set, 1)
            def stats_of(g):
                for i in range(*STAT_GROUPS[g]):
                    r = ROWS[i]
                    for n, (i0, i1) in enumerate(X_LOADS):
                        if i == i0:
                            dve.wait_ge(x_in[n], 16)
                    step(dve.bn_stats(stats[0:r, i % 2, :], x_sb[0:r, i, :]))
                    last = dve.bn_aggr(mv[0:r, i, :], stats[0:r, i % 2, :])
                last.then_inc(stat_done, 1)

            def one_over_std(g):
                i0, i1 = STAT_GROUPS[g]
                dve.wait_ge(std_done, g + 1)
                step(dve.reciprocal(rstd[:, i0:i1], rstd[:, i0:i1]))

            def layer_norm(i):
                r = ROWS[i]
                if i >= 2:
                    dve.wait_ge(t_done, i - 1)
                dve.tensor_scalar(xn[0:r, i % 2], x_sb[0:r, i, :], mv[0:r, i, 0:1], rstd[0:r, i:i + 1],
                                  ALU.subtract, ALU.mult).then_inc(xn_ready, 1)

            def k_feature(i):
                r = ROWS[i]
                dve.wait_ge(ek_ready, i + 1)
                step(dve.tensor_scalar(ex[0:r, i % 2], ex[0:r, i % 2], 1.0, None, ALU.min))
                if i >= 2:
                    dve.wait_ge(acc_done, i - 1)
                dve.scalar_tensor_tensor(out=kf[0:r, i % 2], in0=ps[0:r, K_BANK + i % 2, :], scalar=0.0,
                                         in1=ex[0:r, i % 2], op0=ALU.max, op1=ALU.add).then_inc(kf_ready, 1)

            def low_T(i, high_done, dest, ready):
                dve.wait_ge(high_done, i + 1)
                dve.tensor_tensor(dest[1][:, :, cols(i)], ps[:, T_BANK + i % 2, :].rearrange(
                    "p (k n) -> p k n", k=KC)[:, :, 0:ROWS[i]], dest[0][:, :, cols(i)].bitcast(F32),
                    ALU.subtract).then_inc(ready, 1)

            stats_of(0)
            one_over_std(0)
            layer_norm(0)
            layer_norm(1)
            dve.wait_ge(wh_ready, 1)
            dve.tensor_tensor(w_of(K_, 1)[:, :, :], raw_w[:, 0], w_of(K_, 0)[:, :, :].bitcast(F32),
                              ALU.subtract).then_inc(wk_ready, 1)
            low_T(0, th_ready, xnT, xnT_ready)
            low_T(1, th_ready, xnT, xnT_ready)
            stats_of(1)
            one_over_std(1)
            layer_norm(2)
            layer_norm(3)
            stats_of(2)
            one_over_std(2)
            for s in range(2, NT + 2):
                if s < NT:
                    low_T(s, th_ready, xnT, xnT_ready)
                if s + 2 < NT:
                    layer_norm(s + 2)
                k_feature(s - 2)

            dve.wait_ge(edge_in, 32)
            step(dve.tensor_copy(edge_f[:, :, :], edge_i[:, :, :]))
            dve.tensor_reduce(rng[:, 0:1], edge_f[:, 1, :], AX_X, ALU.min)
            dve.tensor_reduce(rng[:, 1:2], edge_f[:, 1, :], AX_X, ALU.max).then_inc(e_f32, 1)
            dve.wait_ge(acc_done, NT)
            dve.wait_ge(kv_zero, 1)
            acc = ps[:, ACC_BANK:ACC_BANK + 2, :].rearrange("p b (h n) -> p (b h) n", h=2)
            for h in range(2):
                part = slice(HEAD * h, HEAD * h + HEAD)
                dve.tensor_copy(kvb[part, :, part], acc[part, :, part])
                dve.tensor_copy(kvb[part, :, P + h:P + h + 1], acc[part, :, P:P + 1]).then_inc(kvb_ready, 1)
            dve.wait_ge(e_t, 1)
            dve.tensor_copy(edge[0:UK, :, :, :].rearrange("p a k m -> p (a k m)"),
                            ps[0:UK, V_BANK, 0:2 * COLS * UNITS]).then_inc(e_copied, 1)

            dve.wait_ge(e_bc, 1)
            dve.wait_ge(consts, 6)
            lowest, highest = ps[0:NT, V_BANK + 1, 0:UNITS], ps[0:NT, V_BANK + 1, UNITS:2 * UNITS]
            step(dve.tensor_scalar(wcol[:, 0:1], thr[:, :], float(P), None, ALU.add))
            step(dve.tensor_scalar(win[:, 0, :], highest, thr[:, 0:1], None, ALU.is_ge))
            step(dve.scalar_tensor_tensor(out=win[:, 1, :], in0=lowest, scalar=wcol[:, 0:1], in1=win[:, 0, :],
                                          op0=ALU.is_lt, op1=ALU.mult))
            step(dve.tensor_tensor(win[:, 2, :], win[:, 1, :], unit_m[:, 0, :], ALU.mult))
            step(dve.tensor_tensor(win[:, 3, :], win[:, 1, :], unit_m[:, 1, :], ALU.mult))
            step(dve.tensor_reduce(wcol[:, 1:2], win[:, 2, :], AX_X, ALU.min))
            step(dve.tensor_reduce(wcol[:, 2:3], win[:, 3, :], AX_X, ALU.max))
            step(dve.tensor_scalar(wcol[:, 3:4], wcol[:, 1:2], BIG, float(UNITS - 1), ALU.add, ALU.min))
            step(dve.tensor_tensor(wcol[:, 4:5], wcol[:, 2:3], wcol[:, 3:4], ALU.subtract))
            dve.tensor_scalar(wcol[:, 5:6], wcol[:, 4:5], 1.0, None, ALU.max).then_inc(e_win, 1)

            def windows_out():
                dve.wait_ge(e_row, 1)
                step(dve.tensor_copy(wrow[0:1, :, :], ps[0:1, V_BANK, 0:32].rearrange("p (a n) -> p a n", a=2)))
                dve.tensor_copy(wreg[0:1, 0, 0:NT + 1], wrow[0:1, 0, 0:NT + 1])
                dve.tensor_tensor(wreg[0:1, 1, 0:NT], wrow[0:1, 1, 0:NT], wrow[0:1, 0, 0:NT],
                                  ALU.subtract).then_inc(e_reg, 1)

            windows_out()

            def q_feature(g):
                c0, c1 = CHUNKS[g // KC]
                w = c1 - c0
                dve.wait_ge(ek_ready, NT + g + 1)
                step(dve.tensor_scalar(ex[:, g % 2, 0:w], ex[:, g % 2, 0:w], 1.0, None, ALU.min))
                dve.scalar_tensor_tensor(out=qfT[:, g % KC, c0:c1], in0=ps[:, K_BANK + g % 2, 0:w], scalar=0.0,
                                         in1=ex[:, g % 2, 0:w], op0=ALU.max, op1=ALU.add).then_inc(qf_ready, 1)

            def divide(i):
                r = ROWS[i]
                dve.wait_ge(att_done, i + 1)
                step(dve.tensor_scalar(rz[0:r, i % 2], head_rows(i, P + 2)[:, :, P:P + 2], Z_EPS, None, ALU.add))
                step(dve.reciprocal(rz[0:r, i % 2], rz[0:r, i % 2]))
                if i >= 2:
                    dve.wait_ge(yt_done, i - 1)
                dve.tensor_tensor(xn[0:r, i % 2].rearrange("p (c h n) -> p c h n", c=KC, h=2),
                                  head_rows(i, P).rearrange("p c (h n) -> p c h n", h=2),
                                  rz[0:r, i % 2].unsqueeze(3).to_broadcast([r, KC, 2, HEAD]),
                                  ALU.mult).then_inc(y_ready, 1)

            def add_mix(i):
                r = ROWS[i]
                if i == 0:
                    dve.wait_ge(xb_ready, NT)
                dve.wait_ge(mix_done, i + 1)
                dve.tensor_tensor(x_sb[0:r, i, :], ps[0:r, K_BANK + i % 2, :], x_sb[0:r, i, :],
                                  ALU.add).then_inc(mix_added, 1)

            for s in range(NT + MIX_LAG):
                if s < CH * KC:
                    q_feature(s)
                if ATT_LAG <= s < NT + ATT_LAG:
                    divide(s - ATT_LAG)
                if YT_LAG <= s < NT + YT_LAG:
                    low_T(s - YT_LAG, yh_ready, yT, yl_ready)
                if s >= MIX_LAG:
                    add_mix(s - MIX_LAG)

            for i in range(NT):
                r = ROWS[i]
                dve.wait_ge(ph_ready, i + 1)
                dve.tensor_tensor(pn[1][0:r, i, :], ps[0:r, V_BANK + i % 2, :], pn[0][0:r, i, :].bitcast(F32),
                                  ALU.subtract).then_inc(p_ready, 1)
                dve.wait_ge(s_done, i + 1)
                dve.tensor_tensor(self_sb[0:r, i, :], ps[0:r, T_BANK + i % 2, :], b_bc[0:r, :],
                                  ALU.add).then_inc(s_ready, 1)

            dve.wait_ge(gnn_const, 3)

            def hot_rows(d):
                first = dve.value_load(wreg[0:1, 0, d:d + 1], min_val=0, max_val=UNITS * NT)
                last = dve.value_load(wreg[0:1, 0, d + 1:d + 2], min_val=1, max_val=UNITS * NT)
                offset = dve.value_load(wreg[0:1, 1, d:d + 1], min_val=-UNITS * NT, max_val=UNITS)
                with dve.Fori(first, last) as i:
                    m = unit_of(i, offset)
                    slot = ring_slot(i)
                    dve.wait_ge(hot_free, i + 1)
                    dve.tensor_tensor(dst_hot[0:UK, bass.ds(slot, COLS), :],
                                      iota[0:UK, d * P:(d + 1) * P].unsqueeze(1).to_broadcast([UK, COLS, P]),
                                      edge[0:UK, 1, :, bass.ds(m, 1)].to_broadcast([UK, COLS, P]), ALU.is_equal)
                    for k in range(COLS):
                        last_ = dve.tensor_scalar(src_hot[0:UK, bass.ds(slot + k, 1), 0:N], iota[0:UK, 0:N],
                                                  edge[0:UK, 0, k, bass.ds(m, 1)], None, ALU.is_equal)
                    last_.then_inc(hot_ready, 1)

            def degree(d):
                dve.wait_ge(a_copied, d + 1)
                step(dve.tensor_scalar(col[:, 6:7], cnt_sb[:, DEG:DEG + 1], 1.0, None, ALU.max))
                dve.reciprocal(rdeg[:, d:d + 1], col[:, 6:7]).then_inc(deg_ready, 1)

            def counts_low(d, n):
                b0, b1 = AT_GROUPS[n]
                dve.wait_ge(ah_ready, 3 * d + n + 1)
                dve.tensor_tensor(cnt[1][:, b0:b1, :], ps[:, AT_BANK + (3 * d + n) % 2, 0:(b1 - b0) * P].rearrange(
                    "p (k n) -> p k n", k=b1 - b0), cnt[0][:, b0:b1, :].bitcast(F32), ALU.subtract).then_inc(a_ready, 1)

            def normed_low_T(d):
                dve.wait_ge(t2h_ready, d + 1)
                dve.tensor_tensor(xnT[1][:, :, cols(d)], ps[:, T_BANK, :].rearrange(
                    "p (k n) -> p k n", k=KC)[:, :, 0:ROWS[d]], xnT[0][:, :, cols(d)].bitcast(F32),
                    ALU.subtract).then_inc(xn2T_ready, 1)

            def hidden_node(d):
                r = ROWS[d]
                s = d % 2
                dve.wait_ge(msg_done, d + 1)
                dve.wait_ge(deg_ready, d + 1)
                dve.scalar_tensor_tensor(out=kf[0:r, s], in0=ps[0:r, msg_bank(d), :], scalar=rdeg[0:r, d:d + 1],
                                         in1=self_sb[0:r, d, :], op0=ALU.mult, op1=ALU.add).then_inc(g_read, 1)
                dve.wait_ge(g_read, d + 1)
                dve.scalar_tensor_tensor(out=kf[0:r, s], in0=kf[0:r, s], scalar=SLOPE, in1=kf[0:r, s],
                                         op0=ALU.mult, op1=ALU.max).then_inc(h_ready, 1)

            def add_normed(d):
                r = ROWS[d]
                s = d % 2
                dve.wait_ge(h_ready, d + 1)
                dve.wait_ge(ss_ready, d + 1)
                step(dve.tensor_scalar(col[0:r, 8:9], col[0:r, 2 + s:3 + s], NORM_EPS, None, ALU.max))
                step(dve.reciprocal(col[0:r, 9:10], col[0:r, 8:9]))
                step(dve.scalar_tensor_tensor(out=x_sb[0:r, d, :], in0=kf[0:r, s], scalar=col[0:r, 9:10],
                                              in1=x_sb[0:r, d, :], op0=ALU.mult, op1=ALU.add))
                step(dve.bn_stats(stats[0:r, s, :], x_sb[0:r, d, :]))
                dve.bn_aggr(mv2[0:r, s, :], stats[0:r, s, :]).then_inc(st2_ready, 1)

            def layer_norm2(d):
                r = ROWS[d]
                s = d % 2
                dve.wait_ge(st2_ready, d + 1)
                dve.wait_ge(sd2_ready, d + 1)
                step(dve.reciprocal(col[0:r, 10:11], col[0:r, 4 + s:5 + s]))
                if d >= 2:
                    dve.wait_ge(t2_done, d - 1)
                dve.tensor_scalar(xn[0:r, s], x_sb[0:r, d, :], mv2[0:r, s, 0:1], col[0:r, 10:11],
                                  ALU.subtract, ALU.mult).then_inc(xn2_ready, 1)

            def quantize(u):
                s = u % 3
                m = u % 2
                dve.wait_ge(f_in[s], 16 * (u // 3 + 1))
                step(dve.tensor_reduce(scal[:, m, 0, :], raw_f[:, s], AX_X, ALU.add, apply_absolute_value=True))
                step(dve.tensor_scalar(scal[:, m, 0, :], scal[:, m, 0, :], 1.0 / P, Q_EPS, ALU.mult, ALU.add))
                dve.tensor_scalar(scal[:, m, 1, :], scal[:, m, 0, :], 0.5, None, ALU.mult)
                step(dve.tensor_scalar(scal[:, m, 2, :], scal[:, m, 0, :], -0.5, None, ALU.mult))
                if u >= 2:
                    dve.wait_ge(ft_done, u - 1)
                for c in range(KC):
                    dve.tensor_scalar(q_f[:, m, c, :], raw_f[:, s, c, :], scal[:, m, 1, c:c + 1],
                                      scal[:, m, 0, c:c + 1], ALU.is_gt, ALU.mult)
                for c in range(KC):
                    last = dve.tensor_scalar(raw_f[:, s, c, :], raw_f[:, s, c, :], scal[:, m, 2, c:c + 1],
                                             scal[:, m, 0, c:c + 1], ALU.is_lt, ALU.mult)
                last.then_inc(qa_ready, 1)

            def weight_low(u):
                dve.wait_ge(fh_ready, u + 1)
                dve.tensor_tensor(ffn_weight_T(u, 1), ps[:, weight_bank(u), :].rearrange("p (k n) -> p k n", k=KC),
                                  ffn_weight_T(u, 0).bitcast(F32), ALU.subtract).then_inc(fw_ready, 1)

            for s in range(NT + 1):
                if s < NT:
                    hot_rows(s)
                if s >= 1:
                    counts_low(s - 1, 0)
                    counts_low(s - 1, 1)
                    degree(s - 1)
                if s >= 2:
                    hidden_node(s - 2)
                if s >= 1:
                    counts_low(s - 1, 2)
                if s >= 4:
                    normed_low_T(s - 4)
                if s >= 3:
                    layer_norm2(s - 3)
                if s >= 2:
                    add_normed(s - 2)
                if s in EARLY_QUANT:
                    quantize(EARLY_QUANT.index(s))
            for u in range(LEAD):
                weight_low(u)
            normed_low_T(NT - 3)
            hidden_node(NT - 1)
            layer_norm2(NT - 2)
            add_normed(NT - 1)
            layer_norm2(NT - 1)
            normed_low_T(NT - 2)
            for u in range(LEAD, 2 * LEAD):
                quantize(u)
            for j in range(FT):
                for c, (c0, c1) in enumerate(CHUNKS):
                    g = j * CH + c
                    w = c1 - c0
                    dve.wait_ge(gu_done, 2 * g + 2)
                    dve.wait_ge(silu_ready, g + 1)
                    dve.tensor_tensor(act_f[g % 3][:, 0:w], ps[:, PE_GU + CH + c, 0:w], act_f[g % 3][:, 0:w],
                                      ALU.mult).then_inc(hid_ready, 1)
                    if g == 0:
                        normed_low_T(NT - 1)
                    u = next_weight(j, c)
                    if u is not None and u < 2 * FT:
                        weight_low(u)
                        quantize(u + LEAD)
            for u in range(2 * FT, UNITS_W):
                weight_low(u)
                if u + LEAD < UNITS_W:
                    quantize(u + LEAD)
            for i in range(NT):
                r = ROWS[i]
                bank = PE_GU + i % DOWN_A
                dve.wait_ge(down_done, i + 1)
                dve.tensor_tensor(x_sb[0:r, i, :], ps[0:r, bank, :], x_sb[0:r, i, :], ALU.add).then_inc(y_final, 1)

        @block.tensor
        def _(pe):
            def transposes(i, source, bank):
                r = ROWS[i]
                for k in range(KC):
                    last = pe.transpose(ps[:, bank, k * P:k * P + r], source[0:r, k * P:(k + 1) * P], ident[0:r, 0:r])
                return last

            def product(out_, pairs):
                n = 0
                for lhs, rhs in pairs:
                    for ql, qr in PASSES:
                        last = pe.matmul(out_, lhs(ql), rhs(qr), start=(n == 0), stop=(n == 3 * len(pairs) - 1))
                        n += 1
                return last

            def node_rows(i, blk, bank, left=xnT):
                return product(ps[0:ROWS[i], bank, :],
                               [(lambda q, k=k: left[q][:, k, cols(i)], lambda q, k=k: w_of(blk, q)[:, k, :])
                                for k in range(KC)])

            def kv_accumulate(i):
                r = ROWS[i]
                pe.wait_ge(kf_ready, i + 1)
                pe.wait_ge(v_ready, i + 1)
                for pr in range(KC):
                    last = pe.matmul(ps[:, ACC_BANK + pr // 2, 256 * (pr % 2):256 * (pr % 2) + P + 2],
                                     kf[0:r, i % 2, pr * P:(pr + 1) * P], vx[0:r, i % 2, pr, :],
                                     start=(i == 0 and pr % 2 == 0), stop=(i == NT - 1 and pr % 2 == 1), skip_group_check=True)
                last.then_inc(acc_done, 1)

            pe.wait_ge(consts, 1)
            for s in range(NT + 3):
                if s < NT:
                    pe.wait_ge(xn_ready, s + 1)
                    if s >= 2:
                        pe.wait_ge(xnT_ready, s - 1)
                    transposes(s, xn[:, s % 2, :], T_BANK + s % 2).then_inc(t_done, 1)
                if 2 <= s < NT + 2:
                    i = s - 2
                    pe.wait_ge(xnT_ready, i + 1)
                    if i == 0:
                        pe.wait_ge(wk_ready, 1)
                    if i >= 2:
                        pe.wait_ge(kf_ready, i - 1)
                    node_rows(i, K_, K_BANK + i % 2).then_inc(k_done, 1)
                    if i == 0:
                        pe.wait_ge(w_ready, V_)
                    if i >= 2:
                        pe.wait_ge(v_ready, i - 1)
                    last = node_rows(i, V_, V_BANK + i % 2)
                    last.then_inc(v_done, 1)
                if s >= 3:
                    kv_accumulate(s - 3)
            pe.wait_ge(v_done, NT)
            pe.sem_inc(w_used, 2)

            pe.wait_ge(v_ready, NT)
            pe.wait_ge(e_f32, 1)
            for a in range(2):
                for k in range(COLS):
                    at_ = (COLS * a + k) * UNITS
                    last = pe.transpose(ps[0:UK, V_BANK, at_:at_ + UNITS], edge_f[:, a, k * UK:(k + 1) * UK],
                                        ident[0:UNITS, 0:UNITS])
            last.then_inc(e_t, 1)
            for k in range(2):
                last = pe.matmul(ps[0:NT, V_BANK + 1, k * UNITS:(k + 1) * UNITS],
                                 rng[:, k:k + 1].to_broadcast([UNITS, NT]), ident[0:UNITS, 0:UNITS],
                                 start=(k == 0), stop=(k == 1), skip_group_check=True)
            last.then_inc(e_bc, 1)

            def window_rows():
                pe.wait_ge(e_win, 1)
                pe.wait_ge(e_copied, 1)
                pe.matmul(ps[0:1, V_BANK, 0:NT + 1], wcol[:, 5:6], prefix[:, :], start=True, stop=False,
                          skip_group_check=True)
                pe.matmul(ps[0:1, V_BANK, 16:16 + NT], wcol[:, 3:4], ident[0:NT, 0:NT], start=False, stop=True,
                          skip_group_check=True).then_inc(e_row, 1)

            def q_rows(g):
                c0, c1 = CHUNKS[g // KC]
                c = g % KC
                if g >= 2:
                    pe.wait_ge(qf_ready, g - 1)
                product(ps[:, K_BANK + g % 2, 0:c1 - c0],
                        [(lambda q, k=k: w_of(Q_, q)[:, k, c * P:(c + 1) * P], lambda q, k=k: xnT[q][:, k, c0:c1])
                         for k in range(KC)]).then_inc(q_done, 1)

            def attend(i):
                pe.wait_ge(qf_ready, KC * (i // TILES_PER_CHUNK + 1))
                if i == 0:
                    pe.wait_ge(kvb_ready, 2)
                    pe.wait_ge(e_reg, 1)
                if i >= 2:
                    pe.wait_ge(y_ready, i - 1)
                for c in range(KC):
                    last = pe.matmul(head_rows(i, P + 2)[:, c, :], qfT[:, c, cols(i)], kvb[:, c, :],
                                     start=(c % 2 == 0), stop=(c % 2 == 1), skip_group_check=True)
                last.then_inc(att_done, 1)

            pe.wait_ge(w_ready, Q_)
            for s in range(NT + MIX_LAG):
                if s < CH * KC:
                    q_rows(s)
                if s == 1:
                    window_rows()
                if ATT_LAG <= s < NT + ATT_LAG:
                    attend(s - ATT_LAG)
                if YT_LAG <= s < NT + YT_LAG:
                    i = s - YT_LAG
                    pe.wait_ge(y_ready, i + 1)
                    if i >= 2:
                        pe.wait_ge(yl_ready, i - 1)
                    transposes(i, xn[:, i % 2, :], T_BANK + i % 2).then_inc(yt_done, 1)
                if s == CH * KC:
                    pe.wait_ge(q_done, CH * KC)
                    pe.sem_inc(w_used, 1)
                    pe.wait_ge(w_ready, PROJ_)
                    pe.wait_ge(qf_ready, CH * KC)
                if s >= MIX_LAG:
                    i = s - MIX_LAG
                    pe.wait_ge(yl_ready, i + 1)
                    if i >= 2:
                        pe.wait_ge(mix_added, i - 1)
                    node_rows(i, PROJ_, K_BANK + i % 2, yT).then_inc(mix_done, 1)
            pe.wait_ge(mix_done, NT)
            pe.sem_inc(w_used, 1)
            pe.wait_ge(w_ready, SELF_)
            pe.wait_ge(yl_ready, NT)
            for i in range(NT):
                if i >= 2:
                    pe.wait_ge(p_ready, i - 1)
                    pe.wait_ge(s_ready, i - 1)
                node_rows(i, NEIGH_, V_BANK + i % 2).then_inc(p_done, 1)
                node_rows(i, SELF_, T_BANK + i % 2).then_inc(s_done, 1)
            pe.wait_ge(s_done, NT)
            pe.sem_inc(w_used, 2)

            def count_edges(d):
                if d == 0:
                    pe.wait_ge(gnn_const, 3)
                    pe.wait_ge(p_ready, NT)
                    pe.sem_inc(hot_free, RING)
                else:
                    pe.wait_ge(a_copied, d)
                for bank in range(3):
                    pe.matmul(ps[:, A_BANK + bank, :], zero16[:, 0:P], zero16[:, :], start=True, stop=False,
                              skip_group_check=True)
                first = pe.value_load(wreg[0:1, 0, d:d + 1], min_val=0, max_val=UNITS * NT)
                last_ = pe.value_load(wreg[0:1, 0, d + 1:d + 2], min_val=1, max_val=UNITS * NT)
                with pe.Fori(first, last_) as i:
                    slot = ring_slot(i)
                    pe.wait_ge(hot_ready, i + 1)
                    for k in range(COLS):
                        for n0 in (0, 512, 1024):
                            n1 = min(n0 + 512, N + 2)
                            hot = pe.matmul(ps[:, A_BANK + n0 // 512, 0:n1 - n0],
                                            dst_hot[0:UK, bass.ds(slot + k, 1), :],
                                            src_hot[0:UK, bass.ds(slot + k, 1), n0:n1],
                                            start=False, stop=False, skip_group_check=True)
                    hot.then_inc(hot_free, 1)
                for bank in range(3):
                    last = pe.matmul(ps[:, A_BANK + bank, 0:2], zero16[:, 0:P], zero16[:, 0:2], start=False, stop=True,
                                     skip_group_check=True)
                last.then_inc(a_done, 1)

            def counts_T(d, n):
                b0, b1 = AT_GROUPS[n]
                pe.wait_ge(a_copied, d + 1)
                if 3 * d + n == 0:
                    pe.wait_ge(mix_added, NT)
                elif 3 * d + n >= 2:
                    pe.wait_ge(a_ready, 3 * d + n - 1)
                for s in range(b0, b1):
                    last = pe.transpose(ps[0:ROWS[s], AT_BANK + (3 * d + n) % 2, (s - b0) * P:(s - b0 + 1) * P],
                                        cnt_sb[:, s * P:s * P + ROWS[s]], ident[:, :])
                last.then_inc(at_done, 1)

            def messages(d):
                if d == 0:
                    pe.wait_ge(mix_added, NT)
                elif d == 1:
                    pe.wait_ge(s_ready, NT)
                else:
                    pe.wait_ge(g_read, d - 1)
                for s in range(NT):
                    for n in range(len(AT_GROUPS)):
                        if s == AT_GROUPS[n][0]:
                            pe.wait_ge(a_ready, 3 * d + n + 1)
                    for q, (ql, qr) in enumerate(PASSES):
                        last = pe.matmul(ps[0:ROWS[d], msg_bank(d), :], cnt[ql][0:ROWS[s], s, 0:ROWS[d]],
                                         pn[qr][0:ROWS[s], s, :], start=(s == 0 and q == 0),
                                         stop=(s == NT - 1 and q == len(PASSES) - 1))
                last.then_inc(msg_done, 1)

            def normed_T(d):
                pe.wait_ge(xn2_ready, d + 1)
                if d == 0:
                    pe.wait_ge(s_ready, NT)
                else:
                    pe.wait_ge(xn2T_ready, d)
                transposes(d, xn[:, d % 2, :], T_BANK).then_inc(t2_done, 1)

            for s in range(NT + 1):
                if s < NT:
                    count_edges(s)
                if s >= 1:
                    counts_T(s - 1, 2)
                    messages(s - 1)
                if s < NT:
                    counts_T(s, 0)
                    counts_T(s, 1)
                if s >= 3:
                    normed_T(s - 3)

            def weight_T(u):
                pe.wait_ge(q_ready, u + 1)
                if u == LEAD:
                    pe.wait_ge(xn2T_ready, NT)
                elif u == LEAD + 1:
                    pe.wait_ge(g_read, NT)
                elif u > LEAD + 1:
                    pe.wait_ge(fw_ready, u - 1)
                for k in range(KC):
                    last = pe.transpose(ps[:, weight_bank(u), k * P:(k + 1) * P], q_f[:, u % 2, k, :], ident[:, :])
                last.then_inc(ft_done, 1)

            def gate_up(j, c):
                c0, c1 = CHUNKS[c]
                g = j * CH + c
                for part in range(2):
                    pe.wait_ge(fw_ready, 2 * j + part + 1)
                    if part == 0 and j > 0:
                        pe.wait_ge(hid_ready, g - CH + 1)
                    elif part == 0:
                        pe.wait_ge(xn2T_ready, min(NT, TILES_PER_CHUNK * (c + 1)))
                        if c == 0:
                            pe.wait_ge(g_read, NT - 1)
                        else:
                            pe.wait_ge(fw_ready, c)
                    last = product(ps[:, PE_GU + part * CH + c, 0:c1 - c0],
                                   [(lambda q, k=k: gu_T(2 * j + part, q)[:, k, :],
                                     lambda q, k=k: xnT[q][:, k, c0:c1]) for k in range(KC)])
                    last.then_inc(gu_done, 1)

            for u in range(LEAD):
                weight_T(u)
            for j in range(FT):
                for c in range(CH):
                    gate_up(j, c)
                    if j == 0 and c < 2:
                        normed_T(NT - 2 + c)
                    u = next_weight(j, c)
                    if u is not None:
                        weight_T(u)
            pe.wait_ge(gu_done, 2 * CH * FT)
            pe.sem_inc(ffn1_done, 1)

            def down(i, j):
                for n, (ql, qr) in enumerate(PASSES):
                    last = pe.matmul(ps[0:ROWS[i], PE_GU + i % DOWN_A, :], hT[ql][:, j, cols(i)], wdT[qr][j][:, :],
                                     start=(j == 0 and n == 0), stop=(j == FT - 1 and n == 2))
                if j == FT - 1:
                    last.then_inc(down_done, 1)

            for j in range(FT):
                pe.wait_ge(fw_ready, 2 * FT + j + 1)
                pe.wait_ge(hl_ready, CH * (j + 1))
                for i in range(DOWN_A):
                    if j == 0:
                        pe.wait_ge(hid_ready, CH * (FT - 1) + i % CH + 1)
                    down(i, j)
                if 2 * FT + j + LEAD < UNITS_W:
                    weight_T(2 * FT + j + LEAD)
            for i in range(DOWN_A, NT):
                pe.wait_ge(y_final, i - DOWN_A + 1)
                for j in range(FT):
                    down(i, j)


_INS = ['x', 'src', 'dst', 'L0_gnn_W_self', 'L0_gnn_W_neigh', 'L0_gnn_b', 'L0_mix_w_qkv', 'L0_mix_w_proj',
        'L0_mix_b_proj', 'L0_ffn_w_gate', 'L0_ffn_w_up', 'L0_ffn_w_down']


def kernel(**inputs):
    import numpy as _np
    import concourse.bacc as _bacc
    from concourse import mybir as _mybir
    from concourse.bass_utils import run_bass_kernel_spmd as _run

    nc = _bacc.Bacc("TRN2", target_bir_lowering=False, num_devices=1)
    arrays, args = {}, []
    for name in _INS:
        a = _np.ascontiguousarray(inputs[name])
        arrays[f"in_{name}"] = a
        args.append(nc.dram_tensor(f"in_{name}", a.shape, _mybir.dt.from_np(a.dtype), kind="ExternalInput").ap())
    args.append(nc.dram_tensor("out_0", (N, D), _mybir.dt.float32, kind="ExternalOutput").ap())
    gnn_mix_ffn_kernel(nc, *args)
    r = _run(nc, [arrays], core_ids=[0])
    return r.results[0]["out_0"]
```

```python
from contextlib import ExitStack

import concourse.bass as bass
from concourse import mybir

F32 = mybir.dt.float32
F32R = mybir.dt.float32r
F16 = mybir.dt.float16
I32 = mybir.dt.int32
ALU = mybir.AluOpType
ACT = mybir.ActivationFunctionType
AX_X = mybir.AxisListType.X

P = 128
N = 1250
D = 512
KC = D // P
NT = (N + P - 1) // P
ROWS = [min(P, N - i * P) for i in range(NT)]
CHUNKS = [(0, 512), (512, 1024), (1024, N)]
CH = len(CHUNKS)
TILES_PER_CHUNK = 512 // P
HEAD = 64
EDGES = 20000
COLS = 2
UK = 125
UNIT = COLS * UK
STEP = 2
ROUND = 2
RING = ROUND * STEP
UNITS = EDGES // UNIT
SRC_W = NT * P
FFN = 1408
FT = FFN // P
UNITS_W = 3 * FT
HIGH_BITS = 12
LN_EPS = 1e-5
Q_EPS = 1e-5
Z_EPS = 1e-6
NORM_EPS = 1e-12
SLOPE = 0.01
BIG = 999.0

PASSES = [(0, 0), (0, 1), (1, 0)]


def gnn_mix_ffn_kernel(nc, x, src, dst, W_self, W_neigh, b, w_qkv, w_proj, b_proj, w_gate, w_up, w_down, out):
    ctx = ExitStack()
    with ctx:
        arena = 16512

        def at(name, shape, dt, offset):
            return nc.alloc_sbuf_tensor_at(name, shape, dt, offset=arena + offset)

        def sem(name):
            return ctx.enter_context(nc.semaphore(name))

        x_sb = at("x_sb", [P, NT, D], F32, 0)
        XT = 20480
        xnT = [at("xnT_h", [P, KC, N], F32R, XT), at("xnT_l", [P, KC, N], F32R, XT + 20000)]
        wdT = [[None] * FT, [None] * FT]
        WB = 60544
        raw_w = at("raw_w", [P, 2, KC, D], F32, WB)
        WS = WB + 16384
        w_hl = [[at(f"w_{'hl'[q]}{s}", [P, KC, D], F32R, WS + 16384 * s + 8192 * q) for q in (0, 1)] for s in range(3)]
        R1 = WS + 3 * 16384
        yT = [at("yT_h", [P, KC, N], F32R, R1), at("yT_l", [P, KC, N], F32R, R1 + 20000)]
        pn = [at("pn_h", [P, NT, D], F32R, R1), at("pn_l", [P, NT, D], F32R, R1 + 20480)]
        R2 = R1 + 40960
        qfT = at("qfT", [P, KC, N], F32, R2)
        self_sb = at("self_sb", [P, NT, D], F32, R2)
        src_hot = at("src_hot", [P, RING * COLS, SRC_W], F16, WB)
        iota = at("iota", [P, SRC_W], F16, WS + 4096)
        zero16 = at("zero16", [P, 512], F16, WS + 6656)
        dst_hot = at("dst_hot", [P, RING * COLS, P], F16, WS + 7680)
        cnt_sb = at("cnt_sb", [P, SRC_W], F32, WS + 9728)
        junk = at("junk", [P, D], F16, WS + 14848)
        cnt = [at("cnt_h", [P, NT, P], F32R, WS + 16384), at("cnt_l", [P, NT, P], F32R, WS + 21504)]
        hT = [at("hT_h", [P, FT, N], F32R, WB), at("hT_l", [P, FT, N], F32R, WB + 55008)]
        WT = WB + 2 * 55008
        C0 = R2 + 20480
        guT = [[at(f"guT_{'hl'[q]}{s}", [P, KC, P], F32R, WT + 4096 * s + 2048 * q) for q in (0, 1)] for s in range(4)]
        first_at = [[WB + 10240, WB + 12288], [WB + 14336, C0 + 6144]]
        guT0 = [[at(f"guT0_{'hl'[q]}{s}", [P, KC, P], F32R, first_at[s][q]) for q in (0, 1)] for s in (0, 1)]
        for j in range(FT):
            base = C0 + 6144 if j == 0 else XT + 4096 * (j - 1) if j < 10 else WT
            for q in (0, 1):
                wdT[q][j] = at(f"wdT_{'hl'[q]}{j}", [P, D], F32R, base + 2048 * q)
        ex = at("ex", [P, 2, D], F32, C0)
        vx = at("vx", [P, 2, KC, P + 2], F32, C0 + 4096)
        kvb = at("kvb", [P, KC, P + 2], F32, C0 + 4096)
        xn = at("xn", [P, 2, D], F32, C0 + 8256)
        kf = at("kf", [P, 2, D], F32, C0 + 12352)
        C1 = C0 + 16448
        b_bc = at("b_bc", [P, D], F32, C1)
        bp_bc = at("bp_bc", [P, D], F32, C1 + 2048)
        raw_f = at("raw_f", [P, 3, KC, P], F32, C0)
        q_f = at("q_f", [P, 2, KC, P], F32, C1)
        edge = at("edge", [P, 2, COLS, UNITS], F32, C1 + 4096)
        ident = at("ident", [P, P], F32, C1 + 5376)
        small = C1 + 5888
        stats = at("stats", [P, 2, 6], F32, small)
        mv = at("mv", [P, NT, 2], F32, small + 64)
        rstd = at("rstd", [P, NT], F32, small + 160)
        mv2 = at("mv2", [P, 2, 2], F32, small + 224)
        col = at("col", [P, 16], F32, small + 256)
        scal = at("scal", [P, 2, 3, KC], F32, small + 320)
        rdeg = at("rdeg", [P, NT], F32, small + 416)
        eps_c = at("eps_c", [P, 1], F32, small + 480)
        pad = at("pad", [P, 1], F32, small + 512)
        rz = at("rz", [P, 2, KC, 2], F32, small + 640)
        act_f = [at(f"act_f{n}", [P, 512], F32, offset)
                 for n, offset in enumerate((C0 + 12352, small + 896, C0 + 10304))]
        E0 = R1 + 20480
        edge_i = at("edge_i", [UNITS, 2, UNIT], I32, E0)
        edge_f = at("edge_f", [UNITS, 2, UNIT], F32, E0 + 2048)
        rng = at("rng", [UNITS, 2], F32, E0 + 4096)
        win = at("win", [NT, 6, UNITS], F32, E0 + 4160)
        wcol = at("wcol", [NT, 8], F32, E0 + 6144)
        prefix = at("prefix", [NT, NT + 1], F32, E0 + 6208)
        unit_m = at("unit_m", [NT, 2, UNITS], F32, E0 + 6272)
        thr = at("thr", [NT, 1], F32, E0 + 6976)
        wrow = at("wrow", [1, 3, 16], F32, E0 + 7008)
        wreg = at("wreg", [1, 3, 16], I32, small + 704)

        ps = ctx.enter_context(nc.psum_tensor("ps", [P, 8, 512], F32))

        x_in = [sem(f"x_in{g}") for g in range(4)]
        raw_in = [sem(f"raw_in{s}") for s in range(2)]
        bias_in = sem("bias_in")
        edge_in = sem("edge_in")
        consts = sem("consts")
        eps_set = sem("eps_set")
        stat_done = sem("stat_done")
        std_done = sem("std_done")
        xn_ready = sem("xn_ready")
        t_done = sem("t_done")
        th_ready = sem("th_ready")
        xnT_ready = sem("xnT_ready")
        wh_ready = sem("wh_ready")
        wkv_ready = sem("wkv_ready")
        w_ready = sem("w_ready")
        w_used = sem("w_used")
        xb_ready = sem("xb_ready")
        k_done, v_done, acc_done = sem("k_done"), sem("v_done"), sem("acc_done")
        ek_ready = sem("ek_ready")
        kf_ready, v_ready = sem("kf_ready"), sem("v_ready")
        kvb_ready = sem("kvb_ready")
        kv_zero = sem("kv_zero")
        e_f32 = sem("e_f32")
        e_t, e_copied, e_bc, e_win, e_row, e_reg = (sem("e_t"), sem("e_copied"), sem("e_bc"), sem("e_win"),
                                                   sem("e_row"), sem("e_reg"))
        q_done, qf_ready = sem("q_done"), sem("qf_ready")
        att_done, y_ready = sem("att_done"), sem("y_ready")
        yt_done, yh_ready, yl_ready = sem("yt_done"), sem("yh_ready"), sem("yl_ready")
        mix_done, mix_added = sem("mix_done"), sem("mix_added")
        p_done, ph_ready, p_ready = sem("p_done"), sem("ph_ready"), sem("p_ready")
        s_done, s_ready = sem("s_done"), sem("s_ready")
        gnn_const = sem("gnn_const")
        hot_free = sem("hot_free")
        hot_ready = sem("hot_ready")
        a_done = sem("a_done")
        a_copied, deg_ready = sem("a_copied"), sem("deg_ready")
        at_done, ah_ready, a_ready = sem("at_done"), sem("ah_ready"), sem("a_ready")
        msg_done, g_read, t_ready, h_ready, ss_ready = (sem("msg_done"), sem("g_read"), sem("t_ready"),
                                                        sem("h_ready"), sem("ss_ready"))
        st2_ready, sd2_ready, rs2_ready, xn2_ready = (sem("st2_ready"), sem("sd2_ready"), sem("rs2_ready"),
                                                     sem("xn2_ready"))
        xn2_last_ready = sem("xn2_last_ready")
        t2_done, t2h_ready, xn2T_ready = sem("t2_done"), sem("t2h_ready"), sem("xn2T_ready")
        f_in = [sem(f"f_in{s}") for s in range(3)]
        qa_ready, q_ready = sem("qa_ready"), sem("q_ready")
        ft_done, fh_ready, fw_ready = sem("ft_done"), sem("fh_ready"), sem("fw_ready")
        gu_done, silu_ready, hid_ready, hh_ready, hl_ready = (sem("gu_done"), sem("silu_ready"), sem("hid_ready"),
                                                             sem("hh_ready"), sem("hl_ready"))
        ffn1_done = sem("ffn1_done")
        down_done, y_final = sem("down_done"), sem("y_final")
        out_done = sem("out_done")
        dve_step, act_step, pool_step = sem("dve_step"), sem("act_step"), sem("pool_step")

        LEAD = 2
        X_LOADS = [(0, 2), (2, 6), (6, NT - 1), (NT - 1, NT)]
        STAT_GROUPS = [(0, 2), (2, 6), (6, NT)]
        K_, V_, Q_, PROJ_, NEIGH_, SELF_ = range(6)
        W_BLOCKS = [w_qkv[:, D:2 * D], w_qkv[:, 2 * D:3 * D], w_qkv[:, 0:D], w_proj, W_neigh, W_self]

        def w_of(block, q):
            return w_hl[block % 3][q]

        T_BANK, K_BANK, V_BANK, ACC_BANK = 0, 2, 4, 6
        ATT_BANK = 4
        A_BANK, AT_BANK = 5, 3
        PE_GU = 2

        def cols(i):
            return slice(i * P, i * P + ROWS[i])

        def counts_ps(width):
            return ps[:, A_BANK:A_BANK + 3, :].rearrange("p b n -> p (b n)")[:, 0:width]

        def msg_bank(d):
            return 2 - d % 2

        def next_weight(j, c):
            if j == 0:
                return LEAD + c - 1 if c >= 1 else None
            return 2 * j + c + LEAD if c < 2 else None

        def split_beside(j, c):
            u = next_weight(j, c)
            return u if u is not None and u < SPLIT_EARLY else None

        def weight_bank(u):
            return A_BANK + 1 + u if u < LEAD else T_BANK + u % 2

        POOL_NORMS = NT - 2
        SPLIT_EARLY = 2 * FT + 1
        EARLY_QUANT = (6, 7)
        DEG = N
        AT_GROUPS = [(0, 4), (4, 8), (8, NT)]

        def head_rows(i, width):
            bank = ATT_BANK + 2 * (i % 2)
            return ps[0:ROWS[i], bank:bank + 2, :].rearrange("p b (h n) -> p (b h) n", h=2)[:, :, 0:width]

        def normed_rows(eng, d):
            r = ROWS[d]
            s = d % 2
            eng.wait_ge(rs2_ready, d + 1)
            if d >= 2:
                eng.wait_ge(t2_done, d - 1)
            eng.tensor_scalar(xn[0:r, s], x_sb[0:r, d, :], mv2[0:r, s, 0:1], col[0:r, 10 + s:11 + s],
                              ALU.subtract, ALU.mult).then_inc(xn2_ready if d < POOL_NORMS else xn2_last_ready, 1)

        def ffn_weight(u):
            if u < 2 * FT:
                w = (w_gate, w_up)[u % 2]
                return w[(u // 2) * P:(u // 2 + 1) * P, :].rearrange("p (k n) -> p k n", k=KC)
            j = u - 2 * FT
            return w_down.rearrange("(c p) f -> p c f", p=P)[:, :, j * P:(j + 1) * P]

        def gu_T(u, q):
            return guT0[u][q] if u < 2 else guT[u % 4][q]

        def ffn_weight_T(u, q):
            if u < 2 * FT:
                return gu_T(u, q)[:, :, :]
            return wdT[q][u - 2 * FT][:, :].rearrange("p (c n) -> p c n", c=KC)

        ATT_LAG, YT_LAG = 5, 7
        MIX_LAG = CH * KC
        WINDOW_ROWS = ATT_LAG - 1

        def unit_of(i, offset, u):
            return nc.s_assert_within(i * RING + offset + u, 0, UNITS - 1, skip_runtime_bounds_check_because=
                                      "a window's first unit is at least 0 and its last at most the last unit")

        def load_start(eng, d):
            return eng.value_load(wreg[0:1, 0, d:d + 1], min_val=0, max_val=UNITS // STEP * NT)

        def load_end(eng, d):
            return eng.value_load(wreg[0:1, 2, d:d + 1], min_val=0, max_val=2 * UNITS // STEP * NT)

        def counts_have_low(starts, d):
            return starts[d + 1] - starts[d] > (2 ** HIGH_BITS - 1) // (RING * UNIT)

        DOWN_A = 6

        block = ctx.enter_context(nc.Block())

        @block.sync
        def _(sp):
            def load_x(g):
                i0, i1 = X_LOADS[g]
                if i1 < NT:
                    sp.dma_start(x_sb[:, i0:i1, :], x[i0 * P:i1 * P, :].rearrange("(i p) n -> p i n", p=P)
                                 ).then_inc(x_in[g], 16)
                else:
                    sp.dma_start(x_sb[0:ROWS[-1], i0, :], x[i0 * P:N, :]).then_inc(x_in[g], 16)

            def load_w(blk):
                sp.dma_start(raw_w[:, blk % 2], W_BLOCKS[blk].rearrange("(k p) n -> p k n", p=P)
                             ).then_inc(raw_in[blk % 2], 16)

            load_x(0)
            load_w(K_)
            load_w(V_)
            for g in range(1, len(X_LOADS)):
                load_x(g)
            sp.dma_start(bp_bc[:, :], b_proj.partition_broadcast(P)).then_inc(bias_in, 16)
            sp.dma_start(b_bc[:, :], b.partition_broadcast(P)).then_inc(bias_in, 16)
            sp.dma_start(edge_i[:, 0, :], src.rearrange("(m e) -> m e", e=UNIT)).then_inc(edge_in, 16)
            sp.dma_start(edge_i[:, 1, :], dst.rearrange("(m e) -> m e", e=UNIT)).then_inc(edge_in, 16)
            for blk in range(2, 6):
                if blk < 4:
                    sp.wait_ge(wkv_ready, blk - 1)
                else:
                    sp.wait_ge(w_ready, blk - 3)
                load_w(blk)
            sp.wait_ge(s_done, NT)
            for u in range(UNITS_W):
                if u >= 3:
                    sp.wait_ge(q_ready, u - 2)
                sp.dma_start(raw_f[:, u % 3], ffn_weight(u)).then_inc(f_in[u % 3], 16)
            for i in range(NT):
                sp.wait_ge(y_final, i + 1)
                sp.dma_start(out[i * P:i * P + ROWS[i], :], x_sb[0:ROWS[i], i, :]).then_inc(out_done, 16)
            sp.wait_ge(out_done, 16 * NT)

        @block.gpsimd
        def _(pool):
            steps = [0]

            def step(ins):
                steps[0] += 1
                ins.then_inc(pool_step, 1)
                pool.wait_ge(pool_step, steps[0])

            step(pool.iota(ident[:, :], pattern=[[1, P]], base=0, channel_multiplier=-1,
                           allow_small_or_imprecise_dtypes=True))
            pool.tensor_scalar(ident[:, :], ident[:, :], 0.0, None, ALU.is_equal).then_inc(consts, 1)
            pool.memset(vx[:, :, :, P:P + 2], 1.0).then_inc(consts, 1)
            step(pool.iota(prefix[:, :], pattern=[[1, NT + 1]], base=0, channel_multiplier=-1,
                           allow_small_or_imprecise_dtypes=True))
            pool.tensor_scalar(prefix[:, :], prefix[:, :], 0.0, None, ALU.is_gt).then_inc(consts, 1)
            pool.iota(thr[:, :], pattern=[[0, 1]], base=0, channel_multiplier=P,
                      allow_small_or_imprecise_dtypes=True).then_inc(consts, 1)
            pool.iota(unit_m[:, 0, :], pattern=[[1, UNITS]], base=-int(BIG), channel_multiplier=0,
                      allow_small_or_imprecise_dtypes=True).then_inc(consts, 1)
            pool.iota(unit_m[:, 1, :], pattern=[[1, UNITS]], base=1, channel_multiplier=0,
                      allow_small_or_imprecise_dtypes=True).then_inc(consts, 1)

            def w_low(blk):
                pool.wait_ge(wh_ready, blk + 1)
                pool.tensor_tensor(w_of(blk, 1)[:, :, :], raw_w[:, blk % 2], w_of(blk, 0)[:, :, :].bitcast(F32),
                                   ALU.subtract).then_inc(w_ready, 1)

            w_low(Q_)
            pool.wait_ge(bias_in, 32)
            for i in range(NT):
                pool.wait_ge(xn_ready, i + 1)
                pool.tensor_tensor(x_sb[0:ROWS[i], i, :], x_sb[0:ROWS[i], i, :], bp_bc[0:ROWS[i], :],
                                   ALU.add).then_inc(xb_ready, 1)
            pool.wait_ge(acc_done, NT)
            pool.memset(kvb[:, :, :], 0.0).then_inc(kv_zero, 1)
            w_low(PROJ_)
            w_low(NEIGH_)
            w_low(SELF_)
            pool.wait_ge(w_used, 4)
            pool.iota(iota[:, :], pattern=[[1, SRC_W]], base=0, channel_multiplier=0,
                      allow_small_or_imprecise_dtypes=True).then_inc(gnn_const, 1)
            pool.memset(zero16[:, :], 0.0).then_inc(gnn_const, 1)
            pool.wait_ge(w_ready, SELF_ - 1)
            pool.memset(src_hot[:, :, N:SRC_W], 1.0).then_inc(gnn_const, 1)

            def quant_diff(u):
                pool.wait_ge(qa_ready, u + 1)
                if u >= 2:
                    pool.wait_ge(ft_done, u - 1)
                pool.tensor_tensor(q_f[:, u % 2], q_f[:, u % 2], raw_f[:, u % 3], ALU.subtract).then_inc(q_ready, 1)

            for s in range(2, NT + 1):
                d = s - 2
                r = ROWS[d]
                if d < POOL_NORMS:
                    pool.wait_ge(g_read, d + 1)
                    pool.tensor_tensor(kf[0:r, d % 2], kf[0:r, d % 2], self_sb[0:r, d, :],
                                       ALU.add).then_inc(t_ready, 1)
                if 0 <= s - 3 < POOL_NORMS:
                    normed_rows(pool, s - 3)
                if s in EARLY_QUANT:
                    quant_diff(EARLY_QUANT.index(s))
            for u in range(LEAD, 2 * LEAD):
                quant_diff(u)
            for j in range(FT):
                for c, (c0, c1) in enumerate(CHUNKS):
                    g = j * CH + c
                    pool.wait_ge(hh_ready, g + 1)
                    pool.tensor_tensor(hT[1][:, j, c0:c1], act_f[g % 3][:, 0:c1 - c0],
                                       hT[0][:, j, c0:c1].bitcast(F32), ALU.subtract).then_inc(hl_ready, 1)
                    if split_beside(j, c) is not None:
                        quant_diff(split_beside(j, c) + LEAD)
            for u in range(SPLIT_EARLY + LEAD, UNITS_W):
                quant_diff(u)

        @block.scalar
        def _(act):
            def w_high(blk):
                act.wait_ge(raw_in[blk % 2], 16 * (blk // 2 + 1))
                if blk >= 3:
                    act.wait_ge(w_used, blk - 2)
                act.activation(w_of(blk, 0)[:, :, :], raw_w[:, blk % 2], ACT.Copy).then_inc(wh_ready, 1)

            def std(g):
                i0, i1 = STAT_GROUPS[g]
                act.wait_ge(stat_done, g + 1)
                act.activation(rstd[:, i0:i1], mv[:, i0:i1, 1], ACT.Sqrt, bias=eps_c[:, 0:1]).then_inc(std_done, 1)

            def high_T(i, done, dest, ready):
                act.wait_ge(done, i + 1)
                act.activation(dest[0][:, :, cols(i)], ps[:, T_BANK + i % 2, :].rearrange(
                    "p (k n) -> p k n", k=KC)[:, :, 0:ROWS[i]], ACT.Copy).then_inc(ready, 1)

            def k_exp(i):
                r = ROWS[i]
                act.wait_ge(k_done, i + 1)
                if i >= 2:
                    act.wait_ge(kf_ready, i - 1)
                act.activation(ex[0:r, i % 2], ps[0:r, K_BANK + i % 2, :], ACT.Exp).then_inc(ek_ready, 1)

            def v_copy(i):
                r = ROWS[i]
                act.wait_ge(v_done, i + 1)
                if i == 0:
                    act.wait_ge(consts, 2)
                if i >= 2:
                    act.wait_ge(acc_done, i - 1)
                act.activation(vx[0:r, i % 2, :, 0:P],
                               ps[0:r, V_BANK + i % 2, :].rearrange("p (h n) -> p h n", h=KC),
                               ACT.Copy).then_inc(v_ready, 1)

            act.wait_ge(eps_set, 1)
            act.activation(col[:, 12:13], eps_c[:, 0:1], ACT.Sqrt)
            std(0)
            w_high(K_)
            high_T(0, t_done, xnT, th_ready)
            high_T(1, t_done, xnT, th_ready)
            w_high(V_)
            std(1)
            std(2)
            for s in range(2, NT + 2):
                if s < NT:
                    high_T(s, t_done, xnT, th_ready)
                if s == 4:
                    w_high(Q_)
                k_exp(s - 2)
                v_copy(s - 2)
            w_high(PROJ_)
            w_high(NEIGH_)
            for s in range(NT + YT_LAG):
                if s < CH * KC:
                    c0, c1 = CHUNKS[s // KC]
                    act.wait_ge(q_done, s + 1)
                    if s >= 2:
                        act.wait_ge(qf_ready, s - 1)
                    act.activation(ex[:, s % 2, 0:c1 - c0], ps[:, K_BANK + s % 2, 0:c1 - c0],
                                   ACT.Exp).then_inc(ek_ready, 1)
                if s == CH * KC:
                    w_high(SELF_)
                if s >= YT_LAG:
                    high_T(s - YT_LAG, yt_done, yT, yh_ready)
            for i in range(NT):
                r = ROWS[i]
                act.wait_ge(p_done, i + 1)
                act.activation(pn[0][0:r, i, :], ps[0:r, V_BANK + i % 2, :], ACT.Copy).then_inc(ph_ready, 1)

            def counts_copy(d):
                act.wait_ge(a_done, d + 1)
                if d >= 1:
                    act.wait_ge(at_done, 3 * d)
                    act.wait_ge(deg_ready, d)
                act.activation(cnt_sb[:, 0:DEG + 1], counts_ps(DEG + 1), ACT.Copy).then_inc(a_copied, 1)

            def counts_high(d, n):
                b0, b1 = AT_GROUPS[n]
                act.wait_ge(at_done, 3 * d + n + 1)
                act.activation(cnt[0][:, b0:b1, :], ps[:, AT_BANK + (3 * d + n) % 2, 0:(b1 - b0) * P].rearrange(
                    "p (k n) -> p k n", k=b1 - b0), ACT.Copy).then_inc(ah_ready, 1)

            def normed_high_T(d):
                act.wait_ge(t2_done, d + 1)
                act.activation(xnT[0][:, :, cols(d)], ps[:, T_BANK, :].rearrange(
                    "p (k n) -> p k n", k=KC)[:, :, 0:ROWS[d]], ACT.Copy).then_inc(t2h_ready, 1)

            def scaled_messages(d):
                r = ROWS[d]
                act.wait_ge(msg_done, d + 1)
                act.wait_ge(deg_ready, d + 1)
                if d >= 2:
                    act.wait_ge(st2_ready, d - 1)
                act.activation(kf[0:r, d % 2], ps[0:r, msg_bank(d), :], ACT.Copy, scale=rdeg[0:r, d:d + 1]
                               ).then_inc(g_read, 1)

            def norm_of(d):
                r = ROWS[d]
                act.wait_ge(h_ready, d + 1)
                act.activation(junk[0:r, :], kf[0:r, d % 2], ACT.Square, accum_out=col[0:r, d % 2:d % 2 + 1]
                               ).then_inc(act_step, 1)
                act.wait_ge(act_step, d + 1)
                act.activation(col[0:r, 2 + d % 2:3 + d % 2], col[0:r, d % 2:d % 2 + 1], ACT.Sqrt).then_inc(ss_ready, 1)

            def std2(d):
                r = ROWS[d]
                act.wait_ge(st2_ready, d + 1)
                act.activation(col[0:r, 4 + d % 2:5 + d % 2], mv2[0:r, d % 2, 1:2], ACT.Sqrt, bias=eps_c[0:r, 0:1]
                               ).then_inc(sd2_ready, 1)

            def weight_high(u):
                act.wait_ge(ft_done, u + 1)
                if u < 2 * FT and u >= 6:
                    act.wait_ge(gu_done, 2 * CH * ((u - 4) // 2) + 2 * CH)
                if u == 2 * FT + 1:
                    act.wait_ge(ffn1_done, 1)
                act.activation(ffn_weight_T(u, 0), ps[:, weight_bank(u), :].rearrange("p (k n) -> p k n", k=KC),
                               ACT.Copy).then_inc(fh_ready, 1)

            for s in range(NT + 1):
                if s >= 2:
                    norm_of(s - 2)
                if s >= 1:
                    counts_high(s - 1, 2)
                if s < NT:
                    counts_copy(s)
                    counts_high(s, 0)
                    counts_high(s, 1)
                if s >= 2:
                    std2(s - 2)
                if s >= 3:
                    normed_high_T(s - 3)
                if s == NT - 1:
                    for u in range(LEAD):
                        weight_high(u)
                if 0 <= s - 1 < POOL_NORMS:
                    scaled_messages(s - 1)

            norm_of(NT - 1)
            std2(NT - 1)
            normed_high_T(NT - 2)
            for j in range(FT):
                for c, (c0, c1) in enumerate(CHUNKS):
                    g = j * CH + c
                    w = c1 - c0
                    act.wait_ge(gu_done, 2 * g + 1)
                    if g >= 3:
                        act.wait_ge(hl_ready, g - 2)
                    act.activation(act_f[g % 3][:, 0:w], ps[:, PE_GU + c, 0:w], ACT.Silu).then_inc(silu_ready, 1)
                    if g == 0:
                        normed_high_T(NT - 1)
                    act.wait_ge(hid_ready, g + 1)
                    act.activation(hT[0][:, j, c0:c1], act_f[g % 3][:, 0:w], ACT.Copy).then_inc(hh_ready, 1)
                    if split_beside(j, c) is not None:
                        weight_high(split_beside(j, c))
            for u in range(SPLIT_EARLY, UNITS_W):
                weight_high(u)

        @block.vector
        def _(dve):
            steps = [0]

            def step(ins):
                steps[0] += 1
                ins.then_inc(dve_step, 1)
                dve.wait_ge(dve_step, steps[0])

            step(dve.memset(mv[:, :, :], 1.0))
            dve.memset(eps_c[:, :], LN_EPS).then_inc(eps_set, 1)
            def stats_of(g):
                for i in range(*STAT_GROUPS[g]):
                    r = ROWS[i]
                    for n, (i0, i1) in enumerate(X_LOADS):
                        if i == i0:
                            dve.wait_ge(x_in[n], 16)
                    step(dve.bn_stats(stats[0:r, i % 2, :], x_sb[0:r, i, :]))
                    last = dve.bn_aggr(mv[0:r, i, :], stats[0:r, i % 2, :])
                last.then_inc(stat_done, 1)

            def one_over_std(g):
                i0, i1 = STAT_GROUPS[g]
                dve.wait_ge(std_done, g + 1)
                step(dve.reciprocal(rstd[:, i0:i1], rstd[:, i0:i1]))

            def layer_norm(i):
                r = ROWS[i]
                if i >= 2:
                    dve.wait_ge(t_done, i - 1)
                dve.tensor_scalar(xn[0:r, i % 2], x_sb[0:r, i, :], mv[0:r, i, 0:1], rstd[0:r, i:i + 1],
                                  ALU.subtract, ALU.mult).then_inc(xn_ready, 1)

            def k_feature(i):
                r = ROWS[i]
                dve.wait_ge(ek_ready, i + 1)
                step(dve.tensor_scalar(ex[0:r, i % 2], ex[0:r, i % 2], 1.0, None, ALU.min))
                if i >= 2:
                    dve.wait_ge(acc_done, i - 1)
                dve.scalar_tensor_tensor(out=kf[0:r, i % 2], in0=ps[0:r, K_BANK + i % 2, :], scalar=0.0,
                                         in1=ex[0:r, i % 2], op0=ALU.max, op1=ALU.add).then_inc(kf_ready, 1)

            def low_T(i, high_done, dest, ready):
                dve.wait_ge(high_done, i + 1)
                dve.tensor_tensor(dest[1][:, :, cols(i)], ps[:, T_BANK + i % 2, :].rearrange(
                    "p (k n) -> p k n", k=KC)[:, :, 0:ROWS[i]], dest[0][:, :, cols(i)].bitcast(F32),
                    ALU.subtract).then_inc(ready, 1)

            stats_of(0)
            one_over_std(0)
            layer_norm(0)
            layer_norm(1)
            low_T(0, th_ready, xnT, xnT_ready)
            low_T(1, th_ready, xnT, xnT_ready)
            for blk in (K_, V_):
                dve.wait_ge(wh_ready, blk + 1)
                dve.tensor_tensor(w_of(blk, 1)[:, :, :], raw_w[:, blk], w_of(blk, 0)[:, :, :].bitcast(F32),
                                  ALU.subtract).then_inc(wkv_ready, 1)
            stats_of(1)
            one_over_std(1)
            layer_norm(2)
            layer_norm(3)
            stats_of(2)
            one_over_std(2)
            for s in range(2, NT + 2):
                if s < NT:
                    low_T(s, th_ready, xnT, xnT_ready)
                if s + 2 < NT:
                    layer_norm(s + 2)
                k_feature(s - 2)

            dve.wait_ge(edge_in, 32)
            step(dve.tensor_copy(edge_f[:, :, :], edge_i[:, :, :]))
            dve.tensor_reduce(rng[:, 0:1], edge_f[:, 1, :], AX_X, ALU.min)
            dve.tensor_reduce(rng[:, 1:2], edge_f[:, 1, :], AX_X, ALU.max).then_inc(e_f32, 1)
            dve.wait_ge(acc_done, NT)
            dve.wait_ge(kv_zero, 1)
            acc = ps[:, ACC_BANK:ACC_BANK + 2, :].rearrange("p b (h n) -> p (b h) n", h=2)
            for h in range(2):
                part = slice(HEAD * h, HEAD * h + HEAD)
                dve.tensor_copy(kvb[part, :, part], acc[part, :, part])
                dve.tensor_copy(kvb[part, :, P + h:P + h + 1], acc[part, :, P:P + 1]).then_inc(kvb_ready, 1)
            dve.wait_ge(e_t, 1)
            dve.tensor_copy(edge[0:UK, :, :, :].rearrange("p a k m -> p (a k m)"),
                            ps[0:UK, V_BANK, 0:2 * COLS * UNITS]).then_inc(e_copied, 1)

            def window_units():
                dve.wait_ge(e_bc, 1)
                dve.wait_ge(consts, 6)
                lowest, highest = ps[0:NT, V_BANK + 1, 0:UNITS], ps[0:NT, V_BANK + 1, UNITS:2 * UNITS]
                step(dve.tensor_scalar(wcol[:, 0:1], thr[:, :], float(P), None, ALU.add))
                step(dve.tensor_scalar(win[:, 0, :], highest, thr[:, 0:1], None, ALU.is_ge))
                step(dve.scalar_tensor_tensor(out=win[:, 1, :], in0=lowest, scalar=wcol[:, 0:1], in1=win[:, 0, :],
                                              op0=ALU.is_lt, op1=ALU.mult))
                step(dve.tensor_tensor(win[:, 2, :], win[:, 1, :], unit_m[:, 0, :], ALU.mult))
                step(dve.tensor_tensor(win[:, 3, :], win[:, 1, :], unit_m[:, 1, :], ALU.mult))
                step(dve.tensor_reduce(wcol[:, 1:2], win[:, 2, :], AX_X, ALU.min))
                step(dve.tensor_reduce(wcol[:, 2:3], win[:, 3, :], AX_X, ALU.max))

            def window_steps():
                step(dve.tensor_scalar(wcol[:, 3:4], wcol[:, 1:2], BIG, float(UNITS - 1), ALU.add, ALU.min))
                step(dve.tensor_tensor(wcol[:, 4:5], wcol[:, 2:3], wcol[:, 3:4], ALU.subtract))
                step(dve.tensor_scalar(wcol[:, 4:5], wcol[:, 4:5], 1.0, None, ALU.max))
                step(dve.tensor_scalar(win[:, 4, 0:UNITS // STEP], unit_m[:, 1, 0:UNITS:STEP], wcol[:, 4:5], None, ALU.is_le))
                step(dve.tensor_reduce(wcol[:, 5:6], win[:, 4, 0:UNITS // STEP], AX_X, ALU.add))
                step(dve.tensor_scalar(wcol[:, 6:7], wcol[:, 5:6], -float(STEP), float(UNITS), ALU.mult, ALU.add))
                step(dve.tensor_scalar(win[:, 5, 0:UNITS // RING], unit_m[:, 1, 0:UNITS // STEP:ROUND], wcol[:, 5:6], None,
                                       ALU.is_le))
                step(dve.tensor_reduce(wcol[:, 7:8], win[:, 5, 0:UNITS // RING], AX_X, ALU.add))
                dve.tensor_tensor(wcol[:, 3:4], wcol[:, 3:4], wcol[:, 6:7], ALU.min).then_inc(e_win, 1)

            def windows_out():
                dve.wait_ge(e_row, 1)
                step(dve.tensor_copy(wrow[0:1, :, :], ps[0:1, V_BANK, 0:48].rearrange("p (a n) -> p a n", a=3)))
                dve.tensor_copy(wreg[0:1, 0, 0:NT + 1], wrow[0:1, 0, 0:NT + 1])
                dve.scalar_tensor_tensor(out=wreg[0:1, 1, 0:NT], in0=wrow[0:1, 0, 0:NT], scalar=-float(RING),
                                         in1=wrow[0:1, 1, 0:NT], op0=ALU.mult, op1=ALU.add)
                dve.scalar_tensor_tensor(out=wreg[0:1, 2, 0:NT], in0=wrow[0:1, 0, 0:NT], scalar=float(ROUND),
                                         in1=wrow[0:1, 2, 0:NT], op0=ALU.mult, op1=ALU.add).then_inc(e_reg, 1)

            def q_feature(g):
                c0, c1 = CHUNKS[g // KC]
                w = c1 - c0
                dve.wait_ge(ek_ready, NT + g + 1)
                step(dve.tensor_scalar(ex[:, g % 2, 0:w], ex[:, g % 2, 0:w], 1.0, None, ALU.min))
                dve.scalar_tensor_tensor(out=qfT[:, g % KC, c0:c1], in0=ps[:, K_BANK + g % 2, 0:w], scalar=0.0,
                                         in1=ex[:, g % 2, 0:w], op0=ALU.max, op1=ALU.add).then_inc(qf_ready, 1)

            def divide(i):
                r = ROWS[i]
                dve.wait_ge(att_done, i + 1)
                step(dve.tensor_scalar(rz[0:r, i % 2], head_rows(i, P + 2)[:, :, P:P + 2], Z_EPS, None, ALU.add))
                step(dve.reciprocal(rz[0:r, i % 2], rz[0:r, i % 2]))
                if i >= 2:
                    dve.wait_ge(yt_done, i - 1)
                dve.tensor_tensor(xn[0:r, i % 2].rearrange("p (c h n) -> p c h n", c=KC, h=2),
                                  head_rows(i, P).rearrange("p c (h n) -> p c h n", h=2),
                                  rz[0:r, i % 2].unsqueeze(3).to_broadcast([r, KC, 2, HEAD]),
                                  ALU.mult).then_inc(y_ready, 1)

            def add_mix(i):
                r = ROWS[i]
                if i == 0:
                    dve.wait_ge(xb_ready, NT)
                dve.wait_ge(mix_done, i + 1)
                dve.tensor_tensor(x_sb[0:r, i, :], ps[0:r, K_BANK + i % 2, :], x_sb[0:r, i, :],
                                  ALU.add).then_inc(mix_added, 1)

            starts, ends, offsets = [], [], []
            for s in range(NT + MIX_LAG):
                if s < CH * KC:
                    q_feature(s)
                    if s == 0:
                        window_units()
                    if s == 1:
                        window_steps()
                    if s == WINDOW_ROWS:
                        windows_out()
                elif s >= MIX_LAG:
                    d = s - MIX_LAG
                    starts.append(load_start(dve, d))
                    ends.append(load_end(dve, d))
                    offsets.append(dve.value_load(wreg[0:1, 1, d:d + 1], min_val=-UNITS * NT, max_val=UNITS))
                if ATT_LAG <= s < NT + ATT_LAG:
                    divide(s - ATT_LAG)
                if YT_LAG <= s < NT + YT_LAG:
                    low_T(s - YT_LAG, yh_ready, yT, yl_ready)
                if s >= MIX_LAG:
                    add_mix(s - MIX_LAG)

            starts.append(load_start(dve, NT))

            def unit_rows(d, i, u):
                m = unit_of(i, offsets[d], u)
                slots = slice(u * COLS, (u + 1) * COLS)
                dve.wait_ge(hot_free, i * RING + (u + 1))
                dve.tensor_tensor(dst_hot[0:UK, slots, :],
                                  iota[0:UK, d * P:(d + 1) * P].unsqueeze(1).to_broadcast([UK, COLS, P]),
                                  edge[0:UK, 1, :, bass.ds(m, 1)].to_broadcast([UK, COLS, P]), ALU.is_equal)
                for k in range(COLS):
                    last = dve.tensor_scalar(src_hot[0:UK, u * COLS + k, 0:N], iota[0:UK, 0:N],
                                             edge[0:UK, 0, k, bass.ds(m, 1)], None, ALU.is_equal)
                last.then_inc(hot_ready, 1)

            def first_round():
                dve.wait_ge(gnn_const, 3)
                for u in range(STEP):
                    unit_rows(0, 0, u)
                with dve.If(ends[0] > 1):
                    for u in range(STEP, RING):
                        unit_rows(0, 0, u)
                with dve.Else():
                    dve.wait_ge(hot_free, RING)
                    dve.memset(pad[:, 0:1], 0.0).then_inc(hot_ready, STEP)

            for i in range(NT):
                r = ROWS[i]
                dve.wait_ge(ph_ready, i + 1)
                dve.tensor_tensor(pn[1][0:r, i, :], ps[0:r, V_BANK + i % 2, :], pn[0][0:r, i, :].bitcast(F32),
                                  ALU.subtract).then_inc(p_ready, 1)
                dve.wait_ge(s_done, i + 1)
                dve.tensor_tensor(self_sb[0:r, i, :], ps[0:r, T_BANK + i % 2, :], b_bc[0:r, :],
                                  ALU.add).then_inc(s_ready, 1)
                if i == NT - 4:
                    first_round()

            def rounds(d, first, last):
                with dve.Fori(first, last) as i:
                    for u in range(STEP):
                        unit_rows(d, i, u)
                    with dve.If(i * ROUND + 1 < ends[d]):
                        for u in range(STEP, RING):
                            unit_rows(d, i, u)
                    with dve.Else():
                        dve.wait_ge(hot_free, i * RING + RING)
                        dve.memset(pad[:, 0:1], 0.0).then_inc(hot_ready, STEP)

            def hot_rows(d):
                if d == 0:
                    with dve.If(starts[1] > 1):
                        rounds(d, 1, starts[1])
                else:
                    rounds(d, starts[d], starts[d + 1])

            def degree(d):
                dve.wait_ge(a_copied, d + 1)
                step(dve.tensor_scalar(col[:, 6:7], cnt_sb[:, DEG:DEG + 1], 1.0, None, ALU.max))
                dve.reciprocal(rdeg[:, d:d + 1], col[:, 6:7]).then_inc(deg_ready, 1)

            def counts_low(d, groups):
                with dve.If(counts_have_low(starts, d)):
                    for n in groups:
                        b0, b1 = AT_GROUPS[n]
                        dve.wait_ge(ah_ready, 3 * d + n + 1)
                        dve.tensor_tensor(cnt[1][:, b0:b1, :],
                                          ps[:, AT_BANK + (3 * d + n) % 2, 0:(b1 - b0) * P].rearrange(
                                              "p (k n) -> p k n", k=b1 - b0),
                                          cnt[0][:, b0:b1, :].bitcast(F32), ALU.subtract).then_inc(a_ready, 1)
                with dve.Else():
                    dve.wait_ge(ah_ready, 3 * d + groups[-1] + 1)
                    dve.sem_inc(a_ready, len(groups))

            def normed_low_T(d):
                dve.wait_ge(t2h_ready, d + 1)
                dve.tensor_tensor(xnT[1][:, :, cols(d)], ps[:, T_BANK, :].rearrange(
                    "p (k n) -> p k n", k=KC)[:, :, 0:ROWS[d]], xnT[0][:, :, cols(d)].bitcast(F32),
                    ALU.subtract).then_inc(xn2T_ready, 1)

            def hidden_node(d):
                r = ROWS[d]
                s = d % 2
                if d >= POOL_NORMS:
                    dve.wait_ge(msg_done, d + 1)
                    dve.wait_ge(deg_ready, d + 1)
                    dve.scalar_tensor_tensor(out=kf[0:r, s], in0=ps[0:r, msg_bank(d), :], scalar=rdeg[0:r, d:d + 1],
                                             in1=self_sb[0:r, d, :], op0=ALU.mult, op1=ALU.add).then_inc(g_read, 1)
                    dve.wait_ge(g_read, d + 1)
                else:
                    dve.wait_ge(t_ready, d + 1)
                dve.scalar_tensor_tensor(out=kf[0:r, s], in0=kf[0:r, s], scalar=SLOPE, in1=kf[0:r, s],
                                         op0=ALU.mult, op1=ALU.max).then_inc(h_ready, 1)

            def add_normed(d):
                r = ROWS[d]
                s = d % 2
                dve.wait_ge(h_ready, d + 1)
                dve.wait_ge(ss_ready, d + 1)
                step(dve.tensor_scalar(col[0:r, 8:9], col[0:r, 2 + s:3 + s], NORM_EPS, None, ALU.max))
                step(dve.reciprocal(col[0:r, 9:10], col[0:r, 8:9]))
                step(dve.scalar_tensor_tensor(out=x_sb[0:r, d, :], in0=kf[0:r, s], scalar=col[0:r, 9:10],
                                              in1=x_sb[0:r, d, :], op0=ALU.mult, op1=ALU.add))
                step(dve.bn_stats(stats[0:r, s, :], x_sb[0:r, d, :]))
                dve.bn_aggr(mv2[0:r, s, :], stats[0:r, s, :]).then_inc(st2_ready, 1)

            def layer_norm2(d):
                r = ROWS[d]
                s = d % 2
                dve.wait_ge(st2_ready, d + 1)
                dve.wait_ge(sd2_ready, d + 1)
                dve.reciprocal(col[0:r, 10 + s:11 + s], col[0:r, 4 + s:5 + s]).then_inc(rs2_ready, 1)
                if d >= POOL_NORMS:
                    normed_rows(dve, d)

            def quantize(u):
                s = u % 3
                m = u % 2
                dve.wait_ge(f_in[s], 16 * (u // 3 + 1))
                step(dve.tensor_reduce(scal[:, m, 0, :], raw_f[:, s], AX_X, ALU.add, apply_absolute_value=True))
                step(dve.tensor_scalar(scal[:, m, 0, :], scal[:, m, 0, :], 1.0 / P, Q_EPS, ALU.mult, ALU.add))
                dve.tensor_scalar(scal[:, m, 1, :], scal[:, m, 0, :], 0.5, None, ALU.mult)
                step(dve.tensor_scalar(scal[:, m, 2, :], scal[:, m, 0, :], -0.5, None, ALU.mult))
                if u >= 2:
                    dve.wait_ge(ft_done, u - 1)
                for c in range(KC):
                    dve.tensor_scalar(q_f[:, m, c, :], raw_f[:, s, c, :], scal[:, m, 1, c:c + 1],
                                      scal[:, m, 0, c:c + 1], ALU.is_gt, ALU.mult)
                for c in range(KC):
                    last = dve.tensor_scalar(raw_f[:, s, c, :], raw_f[:, s, c, :], scal[:, m, 2, c:c + 1],
                                             scal[:, m, 0, c:c + 1], ALU.is_lt, ALU.mult)
                last.then_inc(qa_ready, 1)

            def weight_low(u):
                dve.wait_ge(fh_ready, u + 1)
                dve.tensor_tensor(ffn_weight_T(u, 1), ps[:, weight_bank(u), :].rearrange("p (k n) -> p k n", k=KC),
                                  ffn_weight_T(u, 0).bitcast(F32), ALU.subtract).then_inc(fw_ready, 1)

            for s in range(NT + 1):
                if s < NT:
                    hot_rows(s)
                if s >= 1:
                    counts_low(s - 1, (0, 1))
                    degree(s - 1)
                if s >= 2:
                    hidden_node(s - 2)
                if s == NT:
                    for u in range(LEAD):
                        weight_low(u)
                if s >= 4:
                    normed_low_T(s - 4)
                if s >= 3:
                    layer_norm2(s - 3)
                if s >= 1:
                    counts_low(s - 1, (2,))
                if s >= 2:
                    add_normed(s - 2)
                if s in EARLY_QUANT:
                    quantize(EARLY_QUANT.index(s))
            quantize(LEAD)
            hidden_node(NT - 1)
            layer_norm2(NT - 2)
            normed_low_T(NT - 3)
            add_normed(NT - 1)
            layer_norm2(NT - 1)
            normed_low_T(NT - 2)
            quantize(LEAD + 1)
            for j in range(FT):
                for c, (c0, c1) in enumerate(CHUNKS):
                    g = j * CH + c
                    w = c1 - c0
                    dve.wait_ge(gu_done, 2 * g + 2)
                    dve.wait_ge(silu_ready, g + 1)
                    dve.tensor_tensor(act_f[g % 3][:, 0:w], ps[:, PE_GU + CH + c, 0:w], act_f[g % 3][:, 0:w],
                                      ALU.mult).then_inc(hid_ready, 1)
                    if g == 0:
                        normed_low_T(NT - 1)
                    u = split_beside(j, c)
                    if u is not None:
                        weight_low(u)
                        if u == LEAD + 1:
                            quantize(u + LEAD - 1)
                        if u != LEAD:
                            quantize(u + LEAD)
            for u in range(SPLIT_EARLY, UNITS_W):
                weight_low(u)
                if u + LEAD < UNITS_W:
                    quantize(u + LEAD)
            for i in range(NT):
                r = ROWS[i]
                bank = PE_GU + i % DOWN_A
                dve.wait_ge(down_done, i + 1)
                dve.tensor_tensor(x_sb[0:r, i, :], ps[0:r, bank, :], x_sb[0:r, i, :], ALU.add).then_inc(y_final, 1)

        @block.tensor
        def _(pe):
            def transposes(i, source, bank):
                r = ROWS[i]
                for k in range(KC):
                    last = pe.transpose(ps[:, bank, k * P:k * P + r], source[0:r, k * P:(k + 1) * P], ident[0:r, 0:r])
                return last

            def product(out_, pairs):
                n = 0
                for lhs, rhs in pairs:
                    for ql, qr in PASSES:
                        last = pe.matmul(out_, lhs(ql), rhs(qr), start=(n == 0), stop=(n == 3 * len(pairs) - 1))
                        n += 1
                return last

            def node_rows(i, blk, bank, left=xnT):
                return product(ps[0:ROWS[i], bank, :],
                               [(lambda q, k=k: left[q][:, k, cols(i)], lambda q, k=k: w_of(blk, q)[:, k, :])
                                for k in range(KC)])

            def kv_accumulate(i):
                r = ROWS[i]
                pe.wait_ge(kf_ready, i + 1)
                pe.wait_ge(v_ready, i + 1)
                for pr in range(KC):
                    last = pe.matmul(ps[:, ACC_BANK + pr // 2, 256 * (pr % 2):256 * (pr % 2) + P + 2],
                                     kf[0:r, i % 2, pr * P:(pr + 1) * P], vx[0:r, i % 2, pr, :],
                                     start=(i == 0 and pr % 2 == 0), stop=(i == NT - 1 and pr % 2 == 1), skip_group_check=True)
                last.then_inc(acc_done, 1)

            pe.wait_ge(consts, 1)
            for s in range(NT + 3):
                if 2 <= s < NT + 2:
                    i = s - 2
                    pe.wait_ge(xnT_ready, i + 1)
                    if i == 0:
                        pe.wait_ge(wkv_ready, 1)
                    if i >= 2:
                        pe.wait_ge(kf_ready, i - 1)
                    node_rows(i, K_, K_BANK + i % 2).then_inc(k_done, 1)
                    if i == 0:
                        pe.wait_ge(wkv_ready, 2)
                    if i >= 2:
                        pe.wait_ge(v_ready, i - 1)
                    last = node_rows(i, V_, V_BANK + i % 2)
                    last.then_inc(v_done, 1)
                if s < NT:
                    pe.wait_ge(xn_ready, s + 1)
                    if s >= 2:
                        pe.wait_ge(xnT_ready, s - 1)
                    transposes(s, xn[:, s % 2, :], T_BANK + s % 2).then_inc(t_done, 1)
                if s >= 3:
                    kv_accumulate(s - 3)
            pe.wait_ge(v_done, NT)
            pe.sem_inc(w_used, 2)

            pe.wait_ge(v_ready, NT)
            pe.wait_ge(e_f32, 1)
            for a in range(2):
                for k in range(COLS):
                    at_ = (COLS * a + k) * UNITS
                    last = pe.transpose(ps[0:UK, V_BANK, at_:at_ + UNITS], edge_f[:, a, k * UK:(k + 1) * UK],
                                        ident[0:UNITS, 0:UNITS])
            last.then_inc(e_t, 1)
            for k in range(2):
                last = pe.matmul(ps[0:NT, V_BANK + 1, k * UNITS:(k + 1) * UNITS],
                                 rng[:, k:k + 1].to_broadcast([UNITS, NT]), ident[0:UNITS, 0:UNITS],
                                 start=(k == 0), stop=(k == 1), skip_group_check=True)
            last.then_inc(e_bc, 1)

            def window_rows():
                pe.wait_ge(e_win, 1)
                pe.wait_ge(e_copied, 1)
                pe.matmul(ps[0:1, V_BANK, 0:NT + 1], wcol[:, 7:8], prefix[:, :], start=True, stop=False,
                          skip_group_check=True)
                pe.matmul(ps[0:1, V_BANK, 32:32 + NT], wcol[:, 5:6], ident[0:NT, 0:NT], start=False, stop=False,
                          skip_group_check=True)
                pe.matmul(ps[0:1, V_BANK, 16:16 + NT], wcol[:, 3:4], ident[0:NT, 0:NT], start=False, stop=True,
                          skip_group_check=True).then_inc(e_row, 1)

            def q_rows(g):
                c0, c1 = CHUNKS[g // KC]
                c = g % KC
                if g >= 2:
                    pe.wait_ge(qf_ready, g - 1)
                product(ps[:, K_BANK + g % 2, 0:c1 - c0],
                        [(lambda q, k=k: w_of(Q_, q)[:, k, c * P:(c + 1) * P], lambda q, k=k: xnT[q][:, k, c0:c1])
                         for k in range(KC)]).then_inc(q_done, 1)

            def attend(i):
                pe.wait_ge(qf_ready, KC * (i // TILES_PER_CHUNK + 1))
                if i == 0:
                    pe.wait_ge(kvb_ready, 2)
                    pe.wait_ge(e_reg, 1)
                if i >= 2:
                    pe.wait_ge(y_ready, i - 1)
                for c in range(KC):
                    last = pe.matmul(head_rows(i, P + 2)[:, c, :], qfT[:, c, cols(i)], kvb[:, c, :],
                                     start=(c % 2 == 0), stop=(c % 2 == 1), skip_group_check=True)
                last.then_inc(att_done, 1)

            pe.wait_ge(w_ready, Q_ - 1)
            for s in range(NT + MIX_LAG):
                if s < CH * KC:
                    q_rows(s)
                if s == WINDOW_ROWS:
                    window_rows()
                if ATT_LAG <= s < NT + ATT_LAG:
                    attend(s - ATT_LAG)
                if YT_LAG <= s < NT + YT_LAG:
                    i = s - YT_LAG
                    pe.wait_ge(y_ready, i + 1)
                    if i >= 2:
                        pe.wait_ge(yl_ready, i - 1)
                    transposes(i, xn[:, i % 2, :], T_BANK + i % 2).then_inc(yt_done, 1)
                if s == CH * KC:
                    pe.wait_ge(q_done, CH * KC)
                    pe.sem_inc(w_used, 1)
                    pe.wait_ge(w_ready, PROJ_ - 1)
                    pe.wait_ge(qf_ready, CH * KC)
                if s >= MIX_LAG:
                    i = s - MIX_LAG
                    pe.wait_ge(yl_ready, i + 1)
                    if i >= 2:
                        pe.wait_ge(mix_added, i - 1)
                    node_rows(i, PROJ_, K_BANK + i % 2, yT).then_inc(mix_done, 1)
            pe.wait_ge(mix_done, NT)
            pe.sem_inc(w_used, 1)
            pe.wait_ge(w_ready, SELF_ - 1)
            pe.wait_ge(yl_ready, NT)
            starts, ends = [], []
            pe.sem_inc(hot_free, RING)
            for i in range(NT):
                if i >= 2:
                    pe.wait_ge(p_ready, i - 1)
                    pe.wait_ge(s_ready, i - 1)
                node_rows(i, NEIGH_, V_BANK + i % 2).then_inc(p_done, 1)
                starts.append(load_start(pe, i))
                ends.append(load_end(pe, i))
                node_rows(i, SELF_, T_BANK + i % 2).then_inc(s_done, 1)
            pe.wait_ge(s_done, NT)
            pe.sem_inc(w_used, 2)

            starts.append(load_start(pe, NT))

            def count_unit(i, u):
                pe.wait_ge(hot_ready, i * RING + (u + 1))
                for k in range(u * COLS, (u + 1) * COLS):
                    for n0 in (0, 512, 1024):
                        n1 = min(n0 + 512, N + 2)
                        hot = pe.matmul(ps[:, A_BANK + n0 // 512, 0:n1 - n0], dst_hot[0:UK, k, :],
                                        src_hot[0:UK, k, n0:n1], start=False, stop=False, skip_group_check=True)
                hot.then_inc(hot_free, 1)

            def count_edges(d):
                if d == 0:
                    pe.wait_ge(gnn_const, 3)
                    pe.wait_ge(p_ready, NT)
                else:
                    pe.wait_ge(a_copied, d)
                for bank in range(3):
                    pe.matmul(ps[:, A_BANK + bank, :], zero16[:, 0:P], zero16[:, :], start=True, stop=False,
                              skip_group_check=True)
                with pe.Fori(starts[d], starts[d + 1]) as i:
                    for u in range(STEP):
                        count_unit(i, u)
                    with pe.If(i * ROUND + 1 < ends[d]):
                        for u in range(STEP, RING):
                            count_unit(i, u)
                    with pe.Else():
                        pe.wait_ge(hot_ready, i * RING + RING)
                        pe.matmul(ps[:, A_BANK, 0:2], zero16[:, 0:P], zero16[:, 0:2], start=False, stop=False,
                                  skip_group_check=True).then_inc(hot_free, STEP)
                for bank in range(3):
                    last = pe.matmul(ps[:, A_BANK + bank, 0:2], zero16[:, 0:P], zero16[:, 0:2], start=False, stop=True,
                                     skip_group_check=True)
                last.then_inc(a_done, 1)

            def counts_T(d, n):
                b0, b1 = AT_GROUPS[n]
                pe.wait_ge(a_copied, d + 1)
                if 3 * d + n == 0:
                    pe.wait_ge(mix_added, NT)
                elif 3 * d + n >= 2:
                    pe.wait_ge(a_ready, 3 * d + n - 1)
                for s in range(b0, b1):
                    last = pe.transpose(ps[0:ROWS[s], AT_BANK + (3 * d + n) % 2, (s - b0) * P:(s - b0 + 1) * P],
                                        cnt_sb[:, s * P:s * P + ROWS[s]], ident[:, :])
                last.then_inc(at_done, 1)

            def messages(d):
                def add(s, ql, qr, start=False):
                    pe.matmul(ps[0:ROWS[d], msg_bank(d), :], cnt[ql][0:ROWS[s], s, 0:ROWS[d]],
                              pn[qr][0:ROWS[s], s, :], start=start, stop=False, skip_group_check=True)

                if d == 0:
                    pe.wait_ge(mix_added, NT)
                elif d == 1:
                    pe.wait_ge(s_ready, NT)
                else:
                    pe.wait_ge(g_read, d - 1)
                for s in range(NT):
                    for n in range(len(AT_GROUPS)):
                        if s == AT_GROUPS[n][0]:
                            pe.wait_ge(a_ready, 3 * d + n + 1)
                    for qr in (0, 1):
                        add(s, 0, qr, start=(s == 0 and qr == 0))
                with pe.If(counts_have_low(starts, d)):
                    for s in range(NT):
                        add(s, 1, 0)
                pe.matmul(ps[:, msg_bank(d), 0:2], zero16[:, 0:P], zero16[:, 0:2], start=False, stop=True,
                          skip_group_check=True).then_inc(msg_done, 1)

            def normed_T(d):
                if d < POOL_NORMS:
                    pe.wait_ge(xn2_ready, d + 1)
                else:
                    pe.wait_ge(xn2_last_ready, d - POOL_NORMS + 1)
                if d == 0:
                    pe.wait_ge(s_ready, NT)
                else:
                    pe.wait_ge(xn2T_ready, d)
                transposes(d, xn[:, d % 2, :], T_BANK).then_inc(t2_done, 1)

            def weight_T(u):
                pe.wait_ge(q_ready, u + 1)
                if u == LEAD:
                    pe.wait_ge(xn2T_ready, NT)
                elif u == LEAD + 1:
                    pe.wait_ge(g_read, NT)
                elif u > LEAD + 1:
                    pe.wait_ge(fw_ready, u - 1)
                for k in range(KC):
                    last = pe.transpose(ps[:, weight_bank(u), k * P:(k + 1) * P], q_f[:, u % 2, k, :], ident[:, :])
                last.then_inc(ft_done, 1)

            for s in range(NT + 1):
                if s < NT:
                    count_edges(s)
                if s >= 1:
                    counts_T(s - 1, 2)
                    messages(s - 1)
                if s < NT:
                    counts_T(s, 0)
                    counts_T(s, 1)
                if 3 <= s < NT:
                    normed_T(s - 3)
                if s == NT - 1:
                    pe.wait_ge(a_copied, NT)
                    for u in range(LEAD):
                        weight_T(u)

            def gate_up(j, c):
                c0, c1 = CHUNKS[c]
                g = j * CH + c
                for part in range(2):
                    pe.wait_ge(fw_ready, 2 * j + part + 1)
                    if part == 0 and j > 0:
                        pe.wait_ge(hid_ready, g - CH + 1)
                    elif part == 0:
                        pe.wait_ge(xn2T_ready, min(NT, TILES_PER_CHUNK * (c + 1)))
                        if c == 0:
                            pe.wait_ge(g_read, NT - 1)
                        else:
                            pe.wait_ge(fw_ready, c)
                    last = product(ps[:, PE_GU + part * CH + c, 0:c1 - c0],
                                   [(lambda q, k=k: gu_T(2 * j + part, q)[:, k, :],
                                     lambda q, k=k: xnT[q][:, k, c0:c1]) for k in range(KC)])
                    last.then_inc(gu_done, 1)
                    if part == 0 and g == 0:
                        normed_T(NT - 3)

            for j in range(FT):
                for c in range(CH):
                    gate_up(j, c)
                    if j == 0 and c < 2:
                        normed_T(NT - 2 + c)
                    u = next_weight(j, c)
                    if u is not None:
                        weight_T(u)
            pe.wait_ge(gu_done, 2 * CH * FT)
            pe.sem_inc(ffn1_done, 1)

            def down(i, j):
                for n, (ql, qr) in enumerate(PASSES):
                    last = pe.matmul(ps[0:ROWS[i], PE_GU + i % DOWN_A, :], hT[ql][:, j, cols(i)], wdT[qr][j][:, :],
                                     start=(j == 0 and n == 0), stop=(j == FT - 1 and n == 2))
                if j == FT - 1:
                    last.then_inc(down_done, 1)

            for j in range(FT):
                pe.wait_ge(fw_ready, 2 * FT + j + 1)
                pe.wait_ge(hl_ready, CH * (j + 1))
                for i in range(DOWN_A):
                    if j == 0:
                        pe.wait_ge(hid_ready, CH * (FT - 1) + i % CH + 1)
                    down(i, j)
                if 2 * FT + j + LEAD < UNITS_W:
                    weight_T(2 * FT + j + LEAD)
            for i in range(DOWN_A, NT):
                pe.wait_ge(y_final, i - DOWN_A + 1)
                for j in range(FT):
                    down(i, j)


_INS = ['x', 'src', 'dst', 'L0_gnn_W_self', 'L0_gnn_W_neigh', 'L0_gnn_b', 'L0_mix_w_qkv', 'L0_mix_w_proj',
        'L0_mix_b_proj', 'L0_ffn_w_gate', 'L0_ffn_w_up', 'L0_ffn_w_down']


def kernel(**inputs):
    import numpy as _np
    import concourse.bacc as _bacc
    from concourse import mybir as _mybir
    from concourse.bass_utils import run_bass_kernel_spmd as _run

    nc = _bacc.Bacc("TRN2", target_bir_lowering=False, num_devices=1)
    arrays, args = {}, []
    for name in _INS:
        a = _np.ascontiguousarray(inputs[name])
        arrays[f"in_{name}"] = a
        args.append(nc.dram_tensor(f"in_{name}", a.shape, _mybir.dt.from_np(a.dtype), kind="ExternalInput").ap())
    args.append(nc.dram_tensor("out_0", (N, D), _mybir.dt.float32, kind="ExternalOutput").ap())
    gnn_mix_ffn_kernel(nc, *args)
    r = _run(nc, [arrays], core_ids=[0])
    return r.results[0]["out_0"]
```
